# Optimizing a Trainium2 kernel written in Bass

```python
import numpy as np
import jax
import jax.numpy as jnp

def _softmax(x, axis=-1):
    return jax.nn.softmax(x, axis=axis)

def _gelu(x):
    return jax.nn.gelu(x, approximate=True)

def _silu(x):
    return jax.nn.silu(x)

def _sigmoid(x):
    return jax.nn.sigmoid(x)

def _layernorm(x, axis=-1, eps=1e-05):
    m = jnp.mean(x, axis=axis, keepdims=True)
    v = jnp.var(x, axis=axis, keepdims=True)
    return (x - m) / jnp.sqrt(v + eps)

def _scatter_add(tgt, idx, src, axis=0):
    return tgt.at[idx].add(src)

def _segment_sum(src, seg, n):
    return jax.ops.segment_sum(src, seg, n)
kernel_name = 'mk_gnn_preln_d1_gnn_r8_719f78'

def setup_inputs(seed: int=0):
    np.random.seed(seed)
    _w = jnp.asarray

    def _rec_inputs():
        import jax
        import jax.numpy as jnp
        _gk = jax.random.key(seed)
        x = -0.000202 + 1 * jax.random.normal(jax.random.fold_in(_gk, 1), (12500, 128), jnp.float32)
        _s = jax.random.randint(jax.random.fold_in(_gk, 2), (100000,), 0, 12500, jnp.int32)
        _d = jax.random.randint(jax.random.fold_in(_gk, 3), (100000,), 0, 12500, jnp.int32)
        _loop = jnp.arange(12500, dtype=jnp.int32)
        src = jnp.concatenate([_s, _d, _loop])
        dst = jnp.concatenate([_d, _s, _loop])
        _o = jnp.argsort(dst, stable=True)
        src = src[_o]
        dst = dst[_o]
        edge_attr_128 = -8.513e-05 + 0.999844 * jax.random.normal(jax.random.fold_in(_gk, 12), (212500, 128), jnp.float32)
        edge_weight1 = jax.random.uniform(jax.random.fold_in(_gk, 13), (212500, 1), jnp.float32, 0.0, 0.999998)
        return (x, src, dst, edge_attr_128, edge_weight1)
    x, src, dst, edge_attr_128, edge_weight1 = _rec_inputs()

    def _L0_gnn_setup():
        import jax, jax.numpy as jnp
        import numpy as np
        import math
        NUM_HEADS = 8
        HEAD_DIM = 16
        SCALE = 1.0 / math.sqrt(HEAD_DIM)

        def _segment_softmax(logits, seg, num):
            m = jax.ops.segment_max(logits, seg, num_segments=num)
            m = jax.lax.stop_gradient(jnp.where(jnp.isfinite(m), m, 0.0))
            e = jnp.exp(logits - m[seg])
            den = jax.ops.segment_sum(e, seg, num_segments=num)
            den = jnp.where(den == 0, 1.0, den)
            return e / den[seg]
        key = jax.random.key(seed)
        ks = jax.random.split(key, 9)
        N, E, F = (6250, 80000, 128)
        node_h = jax.random.normal(ks[0], (N, F), jnp.float32)
        edge_h = jax.random.normal(ks[1], (E, F), jnp.float32)
        distance = jax.random.uniform(ks[2], (E, 1), jnp.float32, minval=0.1, maxval=1.0)
        src = jax.random.randint(ks[3], (E,), 0, N, jnp.int32)
        dst = jax.random.randint(ks[4], (E,), 0, N, jnp.int32)

        def lin(k):
            kw, kb = jax.random.split(k)
            W = jax.random.normal(kw, (F, F), jnp.float32) / math.sqrt(F)
            b = jax.random.normal(kb, (F,), jnp.float32) * 0.02
            return (W, b)
        Wq, bq = lin(ks[5])
        Wk, bk = lin(ks[6])
        Wv, bv = lin(ks[7])
        Wo, bo = lin(ks[8])
        lam = jnp.array(1.0, jnp.float32)
        return dict(node_h=node_h, edge_h=edge_h, distance=distance, Wq=Wq, bq=bq, Wk=Wk, bk=bk, Wv=Wv, bv=bv, Wo=Wo, bo=bo, lam=lam, src=src, dst=dst)
    _L0_gnn_all = _L0_gnn_setup()
    _L0_gnn_in = {k: v for k, v in _L0_gnn_all.items() if k in ('Wq', 'bq', 'Wk', 'bk', 'Wv', 'bv', 'Wo', 'bo', 'lam')}
    del _L0_gnn_all
    return {'x': x, 'src': src, 'dst': dst, 'edge_attr_128': edge_attr_128, 'edge_weight1': edge_weight1, 'L0_gnn_Wq': _L0_gnn_in['Wq'], 'L0_gnn_bq': _L0_gnn_in['bq'], 'L0_gnn_Wk': _L0_gnn_in['Wk'], 'L0_gnn_bk': _L0_gnn_in['bk'], 'L0_gnn_Wv': _L0_gnn_in['Wv'], 'L0_gnn_bv': _L0_gnn_in['bv'], 'L0_gnn_Wo': _L0_gnn_in['Wo'], 'L0_gnn_bo': _L0_gnn_in['bo'], 'L0_gnn_lam': _L0_gnn_in['lam']}

def reference(x, src, dst, edge_attr_128, edge_weight1, L0_gnn_Wq, L0_gnn_bq, L0_gnn_Wk, L0_gnn_bk, L0_gnn_Wv, L0_gnn_bv, L0_gnn_Wo, L0_gnn_bo, L0_gnn_lam):
    import jax
    import jax.numpy as jnp

    def _L0_gnn_ref(node_h, edge_h, distance, Wq, bq, Wk, bk, Wv, bv, Wo, bo, lam, src, dst):
        import jax, jax.numpy as jnp
        import numpy as np
        import math
        NUM_HEADS = 8
        HEAD_DIM = 16
        SCALE = 1.0 / math.sqrt(HEAD_DIM)

        def _segment_softmax(logits, seg, num):
            m = jax.ops.segment_max(logits, seg, num_segments=num)
            m = jax.lax.stop_gradient(jnp.where(jnp.isfinite(m), m, 0.0))
            e = jnp.exp(logits - m[seg])
            den = jax.ops.segment_sum(e, seg, num_segments=num)
            den = jnp.where(den == 0, 1.0, den)
            return e / den[seg]
        N = node_h.shape[0]
        q = (node_h @ Wq.T + bq).reshape(N, NUM_HEADS, HEAD_DIM)
        k = (edge_h @ Wk.T + bk).reshape(-1, NUM_HEADS, HEAD_DIM)
        v = (node_h @ Wv.T + bv).reshape(N, NUM_HEADS, HEAD_DIM)
        qs, qd = (q[src], q[dst])
        in_m = jnp.sum(qs * k, axis=-1)
        out_m = jnp.sum(qd * k, axis=-1)
        diag_m = jnp.sum(qs * qd, axis=-1)
        att = jnp.power(distance, lam)
        score = (_segment_softmax(in_m * SCALE, dst, N) + _segment_softmax(out_m * SCALE, dst, N) + _segment_softmax(diag_m * SCALE, dst, N)) * att
        h = jax.ops.segment_sum(score[..., None] * v[dst], dst, num_segments=N)
        h = h.reshape(N, NUM_HEADS * HEAD_DIM)
        out = h @ Wo.T + bo
        return jax.nn.leaky_relu(out, negative_slope=0.1)
    h = jnp.maximum(_layernorm(x, axis=-1), 0.0)
    x = x + _L0_gnn_ref(h, edge_attr_128, edge_weight1, L0_gnn_Wq, L0_gnn_bq, L0_gnn_Wk, L0_gnn_bk, L0_gnn_Wv, L0_gnn_bv, L0_gnn_Wo, L0_gnn_bo, L0_gnn_lam, src, dst)
    return x

_drawn_inputs = setup_inputs


def setup_inputs(seed=0):
    import zlib

    import numpy as np

    out = dict(_drawn_inputs(seed))
    spreads = {}
    factors = {'L0_gnn_bq': 40.855, 'L0_gnn_bk': 64.0, 'L0_gnn_bv': 3.508, 'L0_gnn_bo': 5.336}
    for name, (base, spread) in spreads.items():
        noise = np.random.default_rng([zlib.crc32(name.encode()), seed]).standard_normal(out[name].shape)
        drawn = base * np.exp(spread * noise) if base else spread * noise
        out[name] = jnp.asarray(drawn.astype(out[name].dtype))
    for name, factor in factors.items():
        out[name] = (out[name] * factor).astype(out[name].dtype)
    return out
```

```python
from contextlib import ExitStack

import concourse.bass as bass
from concourse import mybir

ALU = mybir.AluOpType
ACT = mybir.ActivationFunctionType
AX_X = mybir.AxisListType.X
F32 = mybir.dt.float32
I32 = mybir.dt.int32

P = 128
N, E, F = 12500, 212500, 128
H, D = 8, 16
SCALE = 1.0 / D ** 0.5
EPS = 1e-5
SLOPE = 0.1
NT = -(-N // P)
NPAD = P * NT
HALF = NT // 14
NSTEP = NT // HALF
NCH = -(-E // (P * P))
T = NCH * P
EPAD = P * T
SUP = 16
NSUP = P // SUP
GRP = 4
NG = SUP // GRP
CH = 3 * H
CPS = CH // NSUP
W1 = P + 1
ROW = 3 * CH
BIG = 1e30


def need(eng, sem, n):
    if not isinstance(n, int) or n > 0:
        eng.wait_ge(sem, n)


def gnn_kernel(nc, x, idx, dst_rows, dst_prev, dst_first, ea, dist, wqvT, bqv, wkT, bk, woT, bo, lam, ident_in,
               iota_in, out):
    q_tab = nc.dram_tensor("q_tab", (NPAD, F), F32, kind="Internal").ap()
    v_tab = nc.dram_tensor("v_tab", (NPAD, F), F32, kind="Internal").ap()
    state = nc.dram_tensor("state", (EPAD, ROW), F32, kind="Internal").ap()
    x_v = x.rearrange("(p t) f -> p (t f)", p=P)
    q_v = q_tab.rearrange("(p t) f -> p (t f)", p=P)
    v_v = v_tab.rearrange("(p t) f -> p (t f)", p=P)
    out_v = out.rearrange("(p t) f -> p (t f)", p=P)
    state_v = state.rearrange("(p t) r -> p (t r)", p=P)

    with ExitStack() as ctx:
        def sb(name, shape, dt=F32):
            return ctx.enter_context(nc.sbuf_tensor(name, shape, dt))

        def sem(name):
            return ctx.enter_context(nc.semaphore(name))

        ident = sb("ident", [P, P])
        wqv_sb = sb("wqv_sb", [P, 2 * F])
        wk_sb = sb("wk_sb", [P, F])
        wo_sb = sb("wo_sb", [P, F])
        bqv_sb = sb("bqv_sb", [P, 2 * F])
        bo_sb = sb("bo_sb", [P, F])
        bk4_sb = sb("bk4_sb", [1, GRP * F])
        ones_sb = sb("ones_sb", [1, P])
        eps_sb = sb("eps_sb", [P, 1])
        lam_sb = sb("lam_sb", [P, 1])
        pen = sb("pen", [P, T])
        att = sb("att", [P, T])
        last_i = sb("last_i", [P, NT + 1], I32)
        has = sb("has", [P, NT])
        fix_i = sb("fix_i", [P, 1], I32)
        whole_pen = sb("whole_pen", [P, 1])
        cont_pen = sb("cont_pen", [P, 1])

        node_pass(nc, locals())
        rows = sb("rows", [P, P, ROW])
        edge_pass(nc, locals(), rows)
        finish_runs(nc, locals(), rows)

        out_pass(nc, locals())


def node_pass(nc, env):
    ident, wqv_sb, wk_sb, wo_sb, bqv_sb, bo_sb, bk4_sb = (env[k] for k in (
        "ident", "wqv_sb", "wk_sb", "wo_sb", "bqv_sb", "bo_sb", "bk4_sb"))
    ones_sb, eps_sb, lam_sb, pen, att, last_i, has, fix_i, whole_pen, cont_pen = (env[k] for k in (
        "ones_sb", "eps_sb", "lam_sb", "pen", "att", "last_i", "has", "fix_i", "whole_pen", "cont_pen"))
    x_v, q_v, v_v, dst_rows, dst_prev, dst_first = (env[k] for k in (
        "x_v", "q_v", "v_v", "dst_rows", "dst_prev", "dst_first"))
    NN = NT + 1
    LB = 11
    NB = NN // LB
    with ExitStack() as ctx:
        def sb(name, shape, dt=F32):
            return ctx.enter_context(nc.sbuf_tensor(name, shape, dt))

        def psum(name, shape):
            return ctx.enter_context(nc.psum_tensor(name, shape, F32))

        def sem(name):
            return ctx.enter_context(nc.semaphore(name))

        xs = sb("xs", [P, 2, HALF, F])
        stats = sb("stats", [P, 2, HALF, 6])
        mv = sb("mv", [P, 2, HALF, 2])
        sd = sb("sd", [P, 2, HALF])
        rstd = sb("rstd", [P, 2, HALF])
        nmr = sb("nmr", [P, 2, HALF])
        hb = sb("hb", [P, 2, HALF, F])
        hT = sb("hT", [P, 2, HALF, P])
        qs = sb("qs", [P, 2, HALF, F])
        vs = sb("vs", [P, 2, HALF, F])
        hT_ps = psum("hT_ps", [P, 8, P])
        qv_ps = psum("qv_ps", [P, 8, 2 * F])

        dst_i = sb("dst_i", [P, 2, T], I32)
        dst_f = sb("dst_f", [P, T])
        prev_f = sb("prev_f", [P, T])
        same = sb("same", [P, T])
        first_i = sb("first_i", [P, T], I32)
        first_f = sb("first_f", [P, T])
        sign_out = sb("sign_out", [P, T])
        dist_sb = sb("dist_sb", [P, T])
        nid = sb("nid", [P, NN + 1])
        nidh = sb("nidh", [P, NN])
        signs = sb("signs", [P, NN])
        tile_f = sb("tile_f", [P, NN])
        tile_i = sb("tile_i", [P, NN], I32)
        tile_b = sb("tile_b", [P, 2, LB], I32)
        rows_i = sb("rows_i", [P, 2, LB, P], I32)
        le = sb("le", [P, LB, P])
        cnt = sb("cnt", [P, NN])
        last_f = sb("last_f", [P, NN])
        nfirst = sb("nfirst", [P, 4])

        consts = sem("consts")
        dve_turns = sem("dve_turns")
        pool_turns = sem("pool_turns")
        made = sem("made")
        x_in = [sem("x_in0"), sem("x_in1")]
        stat_step = sem("stat_step")
        mv_ready = sem("mv_ready")
        sd_ready = sem("sd_ready")
        rstd_ready = sem("rstd_ready")
        nmr_ready = sem("nmr_ready")
        h_ready = sem("h_ready")
        hT_ready = sem("hT_ready")
        hT_copied = sem("hT_copied")
        qv_ready = sem("qv_ready")
        qv_copied = sem("qv_copied")
        q_out = [sem("q_out0"), sem("q_out1")]
        dst_in = sem("dst_in")
        first_in = sem("first_in")
        step = sem("step")
        first_ready = sem("first_ready")
        signs_ready = sem("signs_ready")
        tile_ready = sem("tile_ready")
        batch_ready = sem("batch_ready")
        rows_in = [sem("rows_in0"), sem("rows_in1")]
        rows_used = sem("rows_used")
        le_ready = sem("le_ready")
        att_ready = sem("att_ready")

        block = ctx.enter_context(nc.Block())

        @block.sync
        def _(sp):
            sp.dma_start(dst_i[:, 0, :], dst_rows.rearrange("(p c) i -> p (c i)", p=P)).then_inc(dst_in, 16)
            sp.dma_start(dst_i[:, 1, :], dst_prev).then_inc(dst_in, 16)
            sp.dma_start(first_i[:, :], dst_first.to_broadcast([P, T])).then_inc(first_in, 16)
            sp.dma_start(ident[:, :], env["ident_in"]).then_inc(consts, 16)
            sp.dma_start(nid[:, :], env["iota_in"]).then_inc(consts, 16)
            sp.dma_start(wqv_sb[:, :], env["wqvT"]).then_inc(consts, 16)
            sp.dma_start(bqv_sb[:, :], env["bqv"].to_broadcast([P, 2 * F])).then_inc(consts, 16)
            sp.dma_start(wk_sb[:, :], env["wkT"]).then_inc(consts, 16)
            sp.dma_start(wo_sb[:, :], env["woT"]).then_inc(consts, 16)
            sp.dma_start(bo_sb[:, :], env["bo"].to_broadcast([P, F])).then_inc(consts, 16)
            for g in range(GRP):
                sp.dma_start(bk4_sb[:, g * F:(g + 1) * F], env["bk"]).then_inc(consts, 16)
            sp.dma_start(lam_sb[:, :], env["lam"].to_broadcast([P, 1])).then_inc(consts, 16)
            sp.dma_start(dist_sb[:, :], env["dist"]).then_inc(consts, 16)

            def step_pair(w):
                for b in range(2):
                    k = 2 * w + b
                    need(sp, h_ready, k - 1)
                    sp.dma_start(xs[:, b, :, :], x_v[:, bass.ds(k * HALF * F, HALF * F)]).then_inc(x_in[b], 16)

            def store_pair(w):
                for b in range(2):
                    k = 2 * w + b
                    sp.wait_ge(qv_copied, k + 1)
                    sp.dma_start(q_v[:, bass.ds(k * HALF * F, HALF * F)], qs[:, b, :, :]).then_inc(q_out[b], 16)
                    sp.dma_start(v_v[:, bass.ds(k * HALF * F, HALF * F)], vs[:, b, :, :]).then_inc(q_out[b], 16)

            step_pair(0)
            with sp.Fori(1, NSTEP // 2) as w:
                step_pair(w)
                store_pair(w - 1)
            store_pair(NSTEP // 2 - 1)
            for b in range(2):
                sp.wait_ge(q_out[b], 32 * (NSTEP // 2))
            sp.wait_ge(consts, 16 * 13)

        @block.gpsimd
        def _(pool):
            pool.wait_ge(consts, 16 * 13)
            nc.gpsimd.tensor_tensor(att[:, :], dist_sb[:, :], lam_sb[:, 0:1].to_broadcast([P, T]),
                                    ALU.pow).then_inc(att_ready, 1)

            def batch(m, b):
                pool.wait_ge(batch_ready, m + 1)
                pool.sem_inc(pool_turns, 1)
                for j in range(LB):
                    pool.indirect_dma_start(out=rows_i[:, b, j, :], out_offset=None, in_=dst_rows,
                                            in_offset=bass.IndirectOffsetOnAxis(ap=tile_b[:, b, j:j + 1], axis=0)
                                            ).then_inc(rows_in[b], 16)

            with pool.Fori(0, NB // 2) as m:
                batch(2 * m, 0)
                batch(2 * m + 1, 1)
            if NB % 2:
                batch(NB - 1, 0)
            pool.wait_ge(att_ready, 1)

        @block.scalar
        def _(act):
            def level_one(j0, n):
                for j in range(n):
                    need(act, signs_ready, j0 + j)
                    nc.scalar.activation(sign_out[:, :], first_f[:, :], ACT.Sign, bias=nidh[:, bass.ds(j0 + j, 1)],
                                         scale=-1.0, accum_out=signs[:, bass.ds(j0 + j, 1)]).then_inc(signs_ready, 1)

            def node_step(k, b):
                act.wait_ge(mv_ready, k + 1)
                nc.scalar.activation(sd[:, b, :], mv[:, b, :, 1], ACT.Sqrt, bias=eps_sb[:, 0:1]).then_inc(sd_ready, 1)
                act.wait_ge(nmr_ready, k + 1)
                for j in range(HALF):
                    h = nc.scalar.activation(hb[:, b, j, :], xs[:, b, j, :], ACT.Relu, bias=nmr[:, b, j:j + 1],
                                             scale=rstd[:, b, j:j + 1])
                h.then_inc(h_ready, 1)
                act.wait_ge(hT_ready, k + 1)
                nc.scalar.copy(hT[:, b, :, :], hT_ps[:, 0:HALF, :]).then_inc(hT_copied, 1)

            act.wait_ge(made, 2)
            with act.Fori(0, NSTEP // 2) as w:
                for b in range(2):
                    node_step(2 * w + b, b)
            act.wait_ge(first_ready, 1)
            level_one(0, 3)
            with act.Fori(1, NN // 3) as j:
                level_one(3 * j, 3)

        @block.tensor
        def _(pe):
            def node_step(k, b):
                pe.wait_ge(h_ready, k + 1)
                need(pe, hT_copied, k)
                for j in range(HALF):
                    t = nc.tensor.transpose(hT_ps[:, j, :], hb[:, b, j, :], ident[:, :])
                t.then_inc(hT_ready, 1)
                pe.wait_ge(hT_copied, k + 1)
                need(pe, qv_copied, k)
                for j in range(HALF):
                    m = nc.tensor.matmul(qv_ps[:, j, :], hT[:, b, j, :], wqv_sb[:, :], start=True, stop=True)
                m.then_inc(qv_ready, 1)

            pe.wait_ge(consts, 16 * 13)
            node_step(0, 0)
            node_step(1, 1)
            with pe.Fori(1, NSTEP // 2) as w:
                for b in range(2):
                    node_step(2 * w + b, b)

        @block.vector
        def _(dve):
            nc.vector.memset(eps_sb[:, :], EPS).then_inc(made, 1)
            nc.vector.memset(ones_sb[:, :], 1.0).then_inc(made, 1)

            def normalise(k, b):
                dve.wait_ge(sd_ready, k + 1)
                nc.vector.reciprocal(rstd[:, b, :], sd[:, b, :]).then_inc(rstd_ready, 1)
                dve.wait_ge(rstd_ready, k + 1)
                nc.vector.scalar_tensor_tensor(out=nmr[:, b, :], in0=mv[:, b, :, 0], scalar=-1.0, in1=rstd[:, b, :],
                                               op0=ALU.mult, op1=ALU.mult).then_inc(nmr_ready, 1)

            def node_stats(k, w, b):
                dve.wait_ge(x_in[b], 16 * (w + 1))
                for j in range(HALF):
                    s = nc.vector.bn_stats(stats[:, b, j, :], xs[:, b, j, :])
                s.then_inc(stat_step, 1)
                dve.wait_ge(stat_step, k + 1)
                dve.sem_inc(dve_turns, 1)
                for j in range(HALF):
                    a = nc.vector.bn_aggr(mv[:, b, j, :], stats[:, b, j, :])
                a.then_inc(mv_ready, 1)

            def take_qv(k, w, b):
                dve.wait_ge(qv_ready, k + 1)
                need(dve, q_out[b], 32 * w)
                for o, c0 in ((qs, 0), (vs, F)):
                    c = nc.vector.tensor_tensor(o[:, b, :, :], qv_ps[:, 0:HALF, c0:c0 + F],
                                                bqv_sb[:, None, c0:c0 + F].to_broadcast([P, HALF, F]), ALU.add)
                c.then_inc(qv_copied, 1)

            def pair(w):
                for b in range(2):
                    k = 2 * w + b
                    node_stats(k, w, b)
                    normalise(k, b)
                    take_qv(k, w, b)

            dve.wait_ge(first_in, 16)
            nc.vector.tensor_copy(first_f[:, :], first_i[:, :]).then_inc(step, 1)
            dve.wait_ge(consts, 16 * 13)
            nc.vector.tensor_scalar(nidh[:, :], nid[:, 0:NN], 0.5, None, ALU.add).then_inc(step, 1)
            dve.wait_ge(dst_in, 32)
            nc.vector.tensor_copy(dst_f[:, :], dst_i[:, 0, :]).then_inc(step, 1)
            nc.vector.tensor_copy(prev_f[:, :], dst_i[:, 1, :]).then_inc(step, 1)
            dve.wait_ge(step, 4)
            nc.vector.memset(cnt[:, :], 0.0).then_inc(first_ready, 1)
            nc.vector.tensor_tensor(same[:, :], dst_f[:, :], prev_f[:, :], ALU.is_equal).then_inc(step, 1)
            dve.wait_ge(step, 5)
            nc.vector.tensor_scalar(pen[:, :], same[:, :], -1.0, BIG, ALU.add, ALU.mult).then_inc(step, 1)
            nc.vector.tensor_copy(nfirst[:, 1:2], dst_f[:, 0:1]).then_inc(step, 1)
            dve.wait_ge(step, 7)
            nc.vector.tensor_tensor(prev_f[:, :], dst_f[:, :], nfirst[:, 1:2].to_broadcast([P, T]), ALU.is_equal
                                    ).then_inc(step, 1)
            dve.wait_ge(step, 8)
            nc.vector.tensor_reduce(nfirst[:, 0:1], prev_f[:, :], AX_X, ALU.add).then_inc(step, 1)
            nc.vector.tensor_copy(cont_pen[:, :], pen[:, 0:1]).then_inc(step, 1)
            dve.wait_ge(step, 10)
            nc.vector.tensor_scalar(nfirst[:, 2:3], nfirst[:, 0:1], float(T), -1.0, ALU.is_equal, ALU.add
                                    ).then_inc(step, 1)
            dve.wait_ge(step, 11)
            nc.vector.scalar_tensor_tensor(out=whole_pen[:, :], in0=nfirst[:, 2:3], scalar=BIG, in1=cont_pen[:, :],
                                           op0=ALU.mult, op1=ALU.add).then_inc(step, 1)
            nc.vector.tensor_tensor(nfirst[:, 3:4], nfirst[:, 0:1], nid[:, NN:NN + 1], ALU.add).then_inc(step, 1)
            dve.wait_ge(step, 13)
            nc.vector.tensor_copy(fix_i[:, :], nfirst[:, 3:4]).then_inc(step, 1)

            pair(0)
            with dve.Fori(1, NSTEP // 2) as w:
                pair(w)

            dve.wait_ge(signs_ready, NN)
            nc.vector.tensor_scalar(tile_f[:, :], signs[:, :], 0.5, T // 2 - 1.0, ALU.mult, ALU.add).then_inc(step, 1)
            dve.wait_ge(step, 15)
            nc.vector.tensor_scalar(tile_f[:, :], tile_f[:, :], 0.0, None, ALU.max).then_inc(step, 1)
            dve.wait_ge(step, 16)
            nc.vector.tensor_copy(tile_i[:, :], tile_f[:, :]).then_inc(step, 1)
            dve.wait_ge(step, 17)

            def hand_over(m, b):
                nc.vector.tensor_copy(tile_b[:, b, :], tile_i[:, bass.ds(m * LB, LB)]).then_inc(batch_ready, 1)

            def count(m, b, done):
                dve.wait_ge(rows_in[b], done)
                need(dve, rows_used, m)
                nc.vector.tensor_tensor(le[:, :, :], rows_i[:, b, :, :],
                                        nid[:, bass.ds(m * LB, LB)].unsqueeze(2).to_broadcast([P, LB, P]), ALU.is_le
                                        ).then_inc(le_ready, 1)
                dve.wait_ge(le_ready, m + 1)
                nc.vector.tensor_reduce(cnt[:, bass.ds(m * LB, LB)], le[:, :, :], AX_X, ALU.add
                                        ).then_inc(rows_used, 1)

            hand_over(0, 0)
            hand_over(1, 1)
            def two_counts(m):
                for b in range(2):
                    count(2 * m + b, b, 16 * LB * (m + 1))
                    hand_over(2 * m + b + 2, b)

            two_counts(0)
            with dve.Fori(1, NB // 2 - 1) as m:
                two_counts(m)
            count(NB - 3, 0, 16 * LB * (NB // 2))
            hand_over(NB - 1, 0)
            count(NB - 2, 1, 16 * LB * (NB // 2))
            count(NB - 1, 0, 16 * LB * (NB // 2 + 1))
            dve.wait_ge(rows_used, NB)
            nc.vector.scalar_tensor_tensor(out=last_f[:, :], in0=tile_f[:, :], scalar=float(P), in1=cnt[:, :],
                                           op0=ALU.mult, op1=ALU.add).then_inc(step, 1)
            dve.wait_ge(step, 18)
            nc.vector.tensor_tensor(has[:, :], last_f[:, 1:NN], last_f[:, 0:NT], ALU.is_gt).then_inc(step, 1)
            nc.vector.tensor_scalar(last_i[:, :], last_f[:, :], -1.0, 0.0, ALU.add, ALU.max).then_inc(step, 1)
            dve.wait_ge(step, 20)


def edge_pass(nc, env, rows):
    ident, wk_sb, bk4_sb, ones_sb, pen, att = (env[k] for k in (
        "ident", "wk_sb", "bk4_sb", "ones_sb", "pen", "att"))
    q_tab, idx, ea, state_v = (env[k] for k in ("q_tab", "idx", "ea", "state_v"))
    with ExitStack() as ctx:
        def sb(name, shape, dt=F32):
            return ctx.enter_context(nc.sbuf_tensor(name, shape, dt))

        def psum(name, shape):
            return ctx.enter_context(nc.psum_tensor(name, shape, F32))

        def sem(name):
            return ctx.enter_context(nc.semaphore(name))

        ea_sb = sb("ea_sb", [P, 2, SUP * P])
        idx_sb = sb("idx_sb", [P, 2, 2 * SUP], I32)
        qsrc = sb("qsrc", [P, NG, GRP * F])
        qdst = sb("qdst", [P, NG, GRP * F])
        prod = sb("prod", [P, 2, 3, GRP * F])
        logits = sb("logits", [P, 2, CH, P])
        staged = sb("staged", [P, CPS, P])
        pen3 = sb("pen3", [P, CPS, W1])
        terms = sb("terms", [P, 4, CPS, W1])
        sums = sb("sums", [P, 3, CPS, W1])
        diffs = sb("diffs", [P, 2, CPS, P])
        shifted = sb("shifted", [P, CPS, P])
        k_ps = psum("k_ps", [P, 2, GRP * F])
        t_ps = psum("t_ps", [P, 4, P])

        ea_in = [sem("ea_in0"), sem("ea_in1")]
        idx_in = [sem("idx_in0"), sem("idx_in1")]
        q_in = [sem(f"q_in{g}") for g in range(NG)]
        k_ready = sem("k_ready")
        prods_ready = sem("prods_ready")
        logits_ready = sem("logits_ready")
        staged_ready = sem("staged_ready")
        turned = sem("turned")
        terms_ready = sem("terms_ready")
        max_ready = sem("max_ready")
        shift_ready = sem("shift_ready")
        diffs_ready = sem("diffs_ready")
        exps_ready = sem("exps_ready")
        weighted_ready = sem("weighted_ready")
        sums_ready = sem("sums_ready")
        rows_ready = sem("rows_ready")
        rows_out = sem("rows_out")
        const_ready = sem("const_ready")
        pool_turns = sem("pool_turns1")

        block = ctx.enter_context(nc.Block())

        @block.sync
        def _(sp):
            def pair(c, h):
                for b in range(2):
                    u = c * NSUP + 2 * h + b
                    need(sp, prods_ready, NG * (u - 1))
                    sp.dma_start(idx_sb[:, b, :], idx[bass.ds(u, 1), :, :].rearrange("a p n -> (a p) n")
                                 ).then_inc(idx_in[b], 16)
                    sp.dma_start(ea_sb[:, b, :], ea[bass.ds(u, 1), :, :].rearrange("a p n -> (a p) n")
                                 ).then_inc(ea_in[b], 16)

            pair(0, 0)
            with sp.Fori(1, NSUP // 2) as h:
                pair(0, h)
            with sp.Fori(1, NCH) as c:
                with sp.Fori(0, NSUP // 2) as h:
                    pair(c, h)

        @block.gpsimd
        def _(pool):
            def pair(c, h):
                for b in range(2):
                    w = c * (NSUP // 2) + h
                    u = 2 * w + b
                    pool.wait_ge(idx_in[b], 16 * (w + 1))
                    for g in range(NG):
                        need(pool, prods_ready, NG * (u - 1) + g + 1)
                        pool.sem_inc(pool_turns, 1)
                        for buf, o in ((qsrc, 0), (qdst, SUP)):
                            for j in range(GRP):
                                at = o + g * GRP + j
                                pool.indirect_dma_start(
                                    out=buf[:, g, j * F:(j + 1) * F], out_offset=None, in_=q_tab,
                                    in_offset=bass.IndirectOffsetOnAxis(ap=idx_sb[:, b, at:at + 1], axis=0)
                                ).then_inc(q_in[g], 16)

            pair(0, 0)
            with pool.Fori(1, NSUP // 2) as h:
                pair(0, h)
            with pool.Fori(1, NCH) as c:
                with pool.Fori(0, NSUP // 2) as h:
                    pair(c, h)

        @block.tensor
        def _(pe):
            def keys(c, h, b, g):
                w = c * (NSUP // 2) + h
                n = NG * (2 * w + b) + g
                if g == 0:
                    pe.wait_ge(ea_in[b], 16 * (w + 1))
                need(pe, prods_ready, n - 1)
                nc.tensor.matmul(k_ps[:, g % 2, :], ones_sb[:, :], bk4_sb[:, :], start=True, stop=False,
                                 skip_group_check=True)
                for j in range(GRP):
                    t = g * GRP + j
                    m = nc.tensor.matmul(k_ps[:, g % 2, j * F:(j + 1) * F], ea_sb[:, b, t * P:(t + 1) * P],
                                         wk_sb[:, :], start=False, stop=True, skip_group_check=True)
                m.then_inc(k_ready, 1)

            def turn(c, h, b):
                v = (c - 1) * NSUP + 2 * h + b
                pe.wait_ge(staged_ready, v + 1)
                for j in range(CPS):
                    t = nc.tensor.transpose(t_ps[:, j, :], staged[:, j, :], ident[:, :])
                t.then_inc(turned, 1)

            def pair(c, h):
                for b in range(2):
                    keys(c, h, b, 0)
                    if not isinstance(c, int) or c > 0:
                        turn(c, h, b)
                    for g in range(1, NG):
                        keys(c, h, b, g)

            pair(0, 0)
            with pe.Fori(1, NSUP // 2) as h:
                pair(0, h)
            with pe.Fori(1, NCH) as c:
                with pe.Fori(0, NSUP // 2) as h:
                    pair(c, h)
            with pe.Fori(0, NSUP // 2) as h:
                for b in range(2):
                    turn(NCH, h, b)

        @block.scalar
        def _(act):
            def softmax(c, h, b):
                s = 2 * h + b
                v = (c - 1) * NSUP + s
                act.wait_ge(logits_ready, NG * NSUP * c)
                nc.scalar.copy(staged[:, :, :],
                               logits[:, bass.ds((c - 1) % 2, 1), bass.ds(s * CPS, CPS), :].rearrange(
                                   "p a c i -> p (a c) i")).then_inc(staged_ready, 1)
                nc.scalar.copy(pen3[:, :, 1:W1],
                               pen[:, None, bass.ds((c - 1) * P, P)].to_broadcast([P, CPS, P]))
                act.wait_ge(rows_ready, v + 1)
                nc.scalar.copy(terms[:, 1:4, :, 0:1].rearrange("p k c o -> p k (c o)"),
                               rows[:, P - 1, :].rearrange("p (k c) -> p k c", k=3)[:, :, bass.ds(s * CPS, CPS)])
                act.wait_ge(turned, v + 1)
                nc.scalar.copy(terms[:, 1, :, 1:W1], t_ps[:, 0:CPS, :]).then_inc(terms_ready, 1)
                act.wait_ge(diffs_ready, v + 1)
                nc.scalar.activation(terms[:, 0:3:2, :, 1:W1], diffs[:, :, :, :], ACT.Exp, scale=SCALE
                                     ).then_inc(exps_ready, 1)
                act.wait_ge(sums_ready, v + 1)
                need(act, rows_out, 16 * (c - 1))
                nc.scalar.copy(
                    rows[:, :, :].rearrange("p i (k c) -> p k c i", k=3)[:, :, bass.ds(s * CPS, CPS), :],
                    sums[:, :, :, 1:W1]).then_inc(rows_ready, 1)

            def store(c):
                act.wait_ge(rows_ready, NSUP * c + 1)
                act.dma_start(state_v[:, bass.ds((c - 1) * P * ROW, P * ROW)],
                              rows[:, :, :].rearrange("p i r -> p (i r)")).then_inc(rows_out, 16)

            act.wait_ge(const_ready, 2)
            with act.Fori(0, NSUP // 2) as h:
                for b in range(2):
                    softmax(1, h, b)
            store(1)
            with act.Fori(2, NCH + 1) as c:
                with act.Fori(0, NSUP // 2) as h:
                    for b in range(2):
                        softmax(c, h, b)
                store(c)
            act.wait_ge(rows_out, 16 * NCH)

        @block.vector
        def _(dve):
            nc.vector.memset(rows[:, P - 1, 0:CH], -BIG)
            nc.vector.memset(rows[:, P - 1, CH:ROW], 0.0).then_inc(rows_ready, 1)
            nc.vector.memset(pen3[:, :, 0:1], -BIG).then_inc(const_ready, 1)
            nc.vector.memset(terms[:, 0, :, 0:1], 0.0).then_inc(const_ready, 1)

            def edges(c, h, b, g):
                u = c * NSUP + 2 * h + b
                n = NG * u + g
                dve.wait_ge(q_in[g], 16 * 2 * GRP * (u + 1))
                need(dve, logits_ready, n - 1)
                nc.vector.tensor_tensor(prod[:, g % 2, 2, :], qsrc[:, g, :], qdst[:, g, :], ALU.mult)
                dve.wait_ge(k_ready, n + 1)
                nc.vector.tensor_tensor(prod[:, g % 2, 0, :], k_ps[:, g % 2, :], qsrc[:, g, :], ALU.mult)
                nc.vector.tensor_tensor(prod[:, g % 2, 1, :], k_ps[:, g % 2, :], qdst[:, g, :], ALU.mult
                                        ).then_inc(prods_ready, 1)
                dve.wait_ge(prods_ready, n + 1)
                for a in range(3):
                    o = logits[:, bass.ds(c % 2, 1), a * H:(a + 1) * H,
                               bass.ds((2 * h + b) * SUP + g * GRP, GRP)].rearrange("p a c r -> p r (a c)")
                    r = nc.vector.tensor_reduce(o, prod[:, g % 2, a, :].rearrange("p (r c d) -> p r c d", r=GRP, d=D),
                                                AX_X, ALU.add)
                r.then_inc(logits_ready, 1)

            def running_max(c, h, b):
                v = (c - 1) * NSUP + 2 * h + b
                dve.wait_ge(terms_ready, v + 1)
                nc.vector.tensor_tensor_scan(sums[:, 0, :, :].rearrange("p c i -> p (c i)"),
                                             pen3[:, :, :].rearrange("p c i -> p (c i)"),
                                             terms[:, 1, :, :].rearrange("p c i -> p (c i)"), -BIG, ALU.add, ALU.max
                                             ).then_inc(max_ready, 1)
                dve.wait_ge(max_ready, v + 1)
                nc.vector.tensor_tensor(shifted[:, :, :], sums[:, 0, :, 0:P], pen3[:, :, 1:W1], ALU.add
                                        ).then_inc(shift_ready, 1)
                nc.vector.tensor_tensor(diffs[:, 1, :, :], terms[:, 1, :, 1:W1], sums[:, 0, :, 1:W1], ALU.subtract)
                dve.wait_ge(shift_ready, v + 1)
                nc.vector.tensor_tensor(diffs[:, 0, :, :], shifted[:, :, :], sums[:, 0, :, 1:W1], ALU.subtract
                                        ).then_inc(diffs_ready, 1)

            def running_sums(c, h, b):
                v = (c - 1) * NSUP + 2 * h + b
                dve.wait_ge(exps_ready, v + 1)
                nc.vector.tensor_tensor(terms[:, 3, :, 1:W1], terms[:, 2, :, 1:W1],
                                        att[:, None, bass.ds((c - 1) * P, P)].to_broadcast([P, CPS, P]), ALU.mult
                                        ).then_inc(weighted_ready, 1)
                dve.wait_ge(weighted_ready, v + 1)
                for k in (1, 2):
                    s = nc.vector.tensor_tensor_scan(sums[:, k, :, :].rearrange("p c i -> p (c i)"),
                                                     terms[:, 0, :, :].rearrange("p c i -> p (c i)"),
                                                     terms[:, k + 1, :, :].rearrange("p c i -> p (c i)"), 0.0,
                                                     ALU.mult, ALU.add)
                s.then_inc(sums_ready, 1)

            def pair(c, h):
                scans = not isinstance(c, int) or c > 0
                for b in range(2):
                    edges(c, h, b, 0)
                    if scans:
                        dve.wait_ge(rows_ready, (c - 1) * NSUP + 2 * h + b + 1)
                        running_max(c, h, b)
                    edges(c, h, b, 1)
                    edges(c, h, b, 2)
                    if scans:
                        running_sums(c, h, b)
                    edges(c, h, b, 3)

            pair(0, 0)
            with dve.Fori(1, NSUP // 2) as h:
                pair(0, h)
            with dve.Fori(1, NCH) as c:
                with dve.Fori(0, NSUP // 2) as h:
                    pair(c, h)
            with dve.Fori(0, NSUP // 2) as h:
                for b in range(2):
                    dve.wait_ge(rows_ready, (NCH - 1) * NSUP + 2 * h + b + 1)
                    running_max(NCH, h, b)
                    running_sums(NCH, h, b)



def finish_runs(nc, env, rows):
    ident, fix_i, whole_pen, cont_pen, state = (env[k] for k in (
        "ident", "fix_i", "whole_pen", "cont_pen", "state"))
    with ExitStack() as ctx:
        def sb(name, shape, dt=F32):
            return ctx.enter_context(nc.sbuf_tensor(name, shape, dt))

        def psum(name, shape):
            return ctx.enter_context(nc.psum_tensor(name, shape, F32))

        def sem(name):
            return ctx.enter_context(nc.semaphore(name))

        pens = sb("pens", [P, 2, CH])
        ends = sb("ends", [CH, 5, P])
        open_ = sb("open_", [CH, 3, W1])
        diff = sb("diff", [CH, 2, P])
        fac = sb("fac", [CH, 2, P])
        scaled = sb("scaled", [CH, 2, P])
        carry_t = sb("carry_t", [CH, 3, P])
        carry = sb("carry", [P, 3, CH])
        fix = sb("fix", [P, 3, CH])
        best = sb("best", [P, CH])
        cdiff = sb("cdiff", [P, 2, CH])
        cfac = sb("cfac", [P, 2, CH])
        part = sb("part", [P, 2, 2, CH])
        fixed = sb("fixed", [P, 3, CH])
        ends_ps = psum("ends_ps", [P, 2, 4, P])
        carry_ps = psum("carry_ps", [P, 4, P])

        fix_in = sem("fix_in")
        fix_out = sem("fix_out")
        pens_ready = sem("pens_ready")
        ends_turned = sem("ends_turned")
        dve_step = sem("dve_step")
        diff_ready = sem("diff_ready")
        fac_ready = sem("fac_ready")
        carry_ready = sem("carry_ready")
        carry_turned = sem("carry_turned")
        cdiff_ready = sem("cdiff_ready")
        cfac_ready = sem("cfac_ready")
        fixed_ready = sem("fixed_ready")
        block = ctx.enter_context(nc.Block())

        @block.gpsimd
        def _(pool):
            pool.indirect_dma_start(out=fix[:, :, :].rearrange("p k c -> p (k c)"), out_offset=None, in_=state,
                                    in_offset=bass.IndirectOffsetOnAxis(ap=fix_i[:, 0:1], axis=0)
                                    ).then_inc(fix_in, 16)
            pool.wait_ge(fixed_ready, 1)
            pool.indirect_dma_start(out=state, out_offset=bass.IndirectOffsetOnAxis(ap=fix_i[:, 0:1], axis=0),
                                    in_=fixed[:, :, :].rearrange("p k c -> p (k c)"), in_offset=None
                                    ).then_inc(fix_out, 16)
            pool.wait_ge(fix_out, 16)

        @block.tensor
        def _(pe):
            for k in range(3):
                nc.tensor.transpose(ends_ps[0:CH, 0, k, :], rows[:, P - 1, k * CH:(k + 1) * CH], ident[:, :])
            pe.wait_ge(pens_ready, 2)
            nc.tensor.transpose(ends_ps[0:CH, 1, 0, :], pens[:, 0, :], ident[:, :])
            nc.tensor.transpose(ends_ps[0:CH, 1, 1, :], pens[:, 1, :], ident[:, :]).then_inc(ends_turned, 1)
            pe.wait_ge(carry_ready, 3)
            for k in range(3):
                t = nc.tensor.transpose(carry_ps[:, k, 0:CH], carry_t[:, k, :], ident[0:CH, 0:CH])
            t.then_inc(carry_turned, 1)

        @block.scalar
        def _(act):
            act.wait_ge(diff_ready, 1)
            nc.scalar.activation(fac[:, :, :], diff[:, :, :], ACT.Exp, scale=SCALE).then_inc(fac_ready, 1)
            act.wait_ge(cdiff_ready, 1)
            nc.scalar.activation(cfac[:, :, :], cdiff[:, :, :], ACT.Exp, scale=SCALE).then_inc(cfac_ready, 1)

        @block.vector
        def _(dve):
            nc.vector.tensor_copy(pens[:, 0, :], whole_pen[:, 0:1].to_broadcast([P, CH])).then_inc(pens_ready, 1)
            nc.vector.tensor_copy(pens[:, 1, :], cont_pen[:, 0:1].to_broadcast([P, CH])).then_inc(pens_ready, 1)
            nc.vector.memset(open_[:, 0, 0:1], -BIG)
            nc.vector.memset(open_[:, 1:3, 0:1], 0.0)
            dve.wait_ge(ends_turned, 1)
            nc.vector.tensor_copy(ends[:, 0:3, :], ends_ps[0:CH, 0, 0:3, :])
            nc.vector.tensor_copy(ends[:, 3:5, :], ends_ps[0:CH, 1, 0:2, :]).then_inc(dve_step, 1)
            dve.wait_ge(dve_step, 1)
            nc.vector.tensor_tensor_scan(open_[:, 0, 1:W1], ends[:, 3, :], ends[:, 0, :], -BIG, ALU.add, ALU.max
                                         ).then_inc(dve_step, 1)
            dve.wait_ge(dve_step, 2)
            nc.vector.tensor_tensor(diff[:, 0, :], open_[:, 0, 0:P], ends[:, 3, :], ALU.add).then_inc(dve_step, 1)
            nc.vector.tensor_tensor(diff[:, 1, :], ends[:, 0, :], open_[:, 0, 1:W1], ALU.subtract)
            dve.wait_ge(dve_step, 3)
            nc.vector.tensor_tensor(diff[:, 0, :], diff[:, 0, :], open_[:, 0, 1:W1], ALU.subtract
                                    ).then_inc(diff_ready, 1)
            dve.wait_ge(fac_ready, 1)
            for k in range(2):
                m = nc.vector.tensor_tensor(scaled[:, k, :], ends[:, 1 + k, :], fac[:, 1, :], ALU.mult)
            m.then_inc(dve_step, 1)
            dve.wait_ge(dve_step, 4)
            for k in range(2):
                m = nc.vector.tensor_tensor_scan(open_[:, 1 + k, 1:W1], fac[:, 0, :], scaled[:, k, :], 0.0, ALU.mult,
                                                 ALU.add)
            m.then_inc(dve_step, 1)
            dve.wait_ge(dve_step, 5)
            nc.vector.tensor_tensor(carry_t[:, 0, :], open_[:, 0, 0:P], ends[:, 4, :], ALU.add
                                    ).then_inc(carry_ready, 1)
            for k in (1, 2):
                nc.vector.tensor_copy(carry_t[:, k, :], open_[:, k, 0:P]).then_inc(carry_ready, 1)
            dve.wait_ge(carry_turned, 1)
            nc.vector.tensor_copy(carry[:, :, :], carry_ps[:, 0:3, 0:CH]).then_inc(dve_step, 1)
            dve.wait_ge(dve_step, 6)
            dve.wait_ge(fix_in, 16)
            nc.vector.tensor_tensor(best[:, :], carry[:, 0, :], fix[:, 0, :], ALU.max).then_inc(dve_step, 1)
            dve.wait_ge(dve_step, 7)
            nc.vector.tensor_tensor(cdiff[:, 0, :], carry[:, 0, :], best[:, :], ALU.subtract)
            nc.vector.tensor_tensor(cdiff[:, 1, :], fix[:, 0, :], best[:, :], ALU.subtract).then_inc(cdiff_ready, 1)
            dve.wait_ge(cfac_ready, 1)
            for k in range(2):
                nc.vector.tensor_tensor(part[:, k, 0, :], carry[:, 1 + k, :], cfac[:, 0, :], ALU.mult)
                m = nc.vector.tensor_tensor(part[:, k, 1, :], fix[:, 1 + k, :], cfac[:, 1, :], ALU.mult)
            m.then_inc(dve_step, 1)
            dve.wait_ge(dve_step, 8)
            nc.vector.tensor_copy(fixed[:, 0, :], best[:, :])
            nc.vector.tensor_tensor(fixed[:, 1:3, :], part[:, :, 0, :], part[:, :, 1, :], ALU.add
                                    ).then_inc(fixed_ready, 1)


def out_pass(nc, env):
    ident, wo_sb, bo_sb, last_i, has, state, x_v, v_v, out_v = (env[k] for k in (
        "ident", "wo_sb", "bo_sb", "last_i", "has", "state", "x_v", "v_v", "out_v"))
    with ExitStack() as ctx:
        def sb(name, shape, dt=F32):
            return ctx.enter_context(nc.sbuf_tensor(name, shape, dt))

        def psum(name, shape):
            return ctx.enter_context(nc.psum_tensor(name, shape, F32))

        def sem(name):
            return ctx.enter_context(nc.semaphore(name))

        xs = sb("xs2", [P, 2, HALF, F])
        vs = sb("vs2", [P, 2, HALF, F])
        last_b = sb("last_b", [P, 2, HALF], I32)
        st = sb("st", [P, 2, HALF, 3, CH])
        rden = sb("rden", [P, HALF, CH])
        ratio = sb("ratio", [P, HALF, CH])
        score = sb("score", [P, HALF, H])
        score_m = sb("score_m", [P, HALF, H])
        hv = sb("hv", [P, 2, HALF, F])
        hvT = sb("hvT", [P, 2, HALF, P])
        z = sb("z", [P, HALF, F])
        y = sb("y", [P, HALF, F])
        res = sb("res", [P, 2, HALF, F])
        hT_ps = psum("hT_ps2", [P, 2, 8, P])
        z_ps = psum("z_ps", [P, 2, 8, P])

        in_sem = [sem("in0"), sem("in1")]
        batch_ready = sem("batch_ready2")
        pool_turns = sem("pool_turns2")
        st_in = [sem("st_in0"), sem("st_in1")]
        step = [sem(f"node_step{i}") for i in range(4)]
        hv_ready = sem("hv_ready")
        hvT_ready = sem("hvT_ready")
        hvT_copied = sem("hvT_copied")
        z_ready = sem("z_ready")
        z_step = sem("z_step")
        y_step = sem("y_step")
        res_ready = sem("res_ready")
        res_out = [sem("res_out0"), sem("res_out1")]
        block = ctx.enter_context(nc.Block())

        @block.sync
        def _(sp):
            def load(w):
                for b in range(2):
                    k = 2 * w + b
                    need(sp, res_ready, k - 1)
                    sp.dma_start(xs[:, b, :, :], x_v[:, bass.ds(k * HALF * F, HALF * F)]).then_inc(in_sem[b], 16)
                    sp.dma_start(vs[:, b, :, :], v_v[:, bass.ds(k * HALF * F, HALF * F)]).then_inc(in_sem[b], 16)

            load(0)
            with sp.Fori(1, NSTEP // 2) as w:
                load(w)

        @block.gpsimd
        def _(pool):
            with pool.Fori(0, NSTEP // 2) as w:
                for b in range(2):
                    pool.wait_ge(batch_ready, 2 * w + b + 1)
                    pool.sem_inc(pool_turns, 1)
                    for j in range(HALF):
                        pool.indirect_dma_start(out=st[:, b, j, :, :].rearrange("p k c -> p (k c)"), out_offset=None,
                                                in_=state,
                                                in_offset=bass.IndirectOffsetOnAxis(ap=last_b[:, b, j:j + 1], axis=0)
                                                ).then_inc(st_in[b], 16)

        @block.tensor
        def _(pe):
            def turn(k, b):
                pe.wait_ge(hv_ready, k + 1)
                for j in range(HALF):
                    t = nc.tensor.transpose(hT_ps[:, b, j, :], hv[:, b, j, :], ident[:, :])
                t.then_inc(hvT_ready, 1)

            def project(k, b):
                pe.wait_ge(hvT_copied, k + 1)
                need(pe, z_step, k - 1)
                for j in range(HALF):
                    m = nc.tensor.matmul(z_ps[:, b, j, :], hvT[:, b, j, :], wo_sb[:, :], start=True, stop=True)
                m.then_inc(z_ready, 1)

            turn(0, 0)
            project(0, 0)
            turn(1, 1)
            project(1, 1)
            with pe.Fori(1, NSTEP // 2) as w:
                for b in range(2):
                    turn(2 * w + b, b)
                    project(2 * w + b, b)

        @block.scalar
        def _(act):
            def copy(k, b):
                act.wait_ge(hvT_ready, k + 1)
                nc.scalar.copy(hvT[:, b, :, :], hT_ps[:, b, 0:HALF, :]).then_inc(hvT_copied, 1)

            def store(k, b):
                act.wait_ge(res_ready, k + 1)
                act.dma_start(out_v[:, bass.ds(k * HALF * F, HALF * F)], res[:, b, :, :]).then_inc(res_out[b], 16)

            copy(0, 0)
            copy(1, 1)
            store(0, 0)
            with act.Fori(1, NSTEP // 2) as w:
                copy(2 * w, 0)
                store(2 * w - 1, 1)
                copy(2 * w + 1, 1)
                store(2 * w, 0)
            store(NSTEP - 1, 1)
            for b in range(2):
                act.wait_ge(res_out[b], 16 * (NSTEP // 2))

        @block.vector
        def _(dve):
            def hand_over(k, b):
                nc.vector.tensor_copy(last_b[:, b, :], last_i[:, bass.ds(k * HALF + 1, HALF)]
                                      ).then_inc(batch_ready, 1)

            def scores(k, w, b):
                dve.wait_ge(st_in[b], 16 * HALF * (w + 1))
                nc.vector.reciprocal(rden[:, :, :], st[:, b, :, 1, :]).then_inc(step[0], 1)
                dve.wait_ge(step[0], k + 1)
                nc.vector.tensor_tensor(ratio[:, :, :], st[:, b, :, 2, :], rden[:, :, :], ALU.mult
                                        ).then_inc(step[1], 1)
                dve.wait_ge(step[1], k + 1)
                nc.vector.tensor_reduce(score[:, :, :], ratio[:, :, :].rearrange("p t (a h) -> p t h a", a=3), AX_X,
                                        ALU.add).then_inc(step[2], 1)
                dve.wait_ge(step[2], k + 1)
                nc.vector.tensor_tensor(score_m[:, :, :], score[:, :, :],
                                        has[:, bass.ds(k * HALF, HALF)].unsqueeze(2).to_broadcast([P, HALF, H]),
                                        ALU.mult).then_inc(step[3], 1)
                dve.wait_ge(step[3], k + 1)
                dve.wait_ge(in_sem[b], 32 * (w + 1))
                nc.vector.tensor_tensor(hv[:, b, :, :].rearrange("p t (h d) -> p (t h) d", h=H),
                                        vs[:, b, :, :].rearrange("p t (h d) -> p (t h) d", h=H),
                                        score_m[:, :, :].rearrange("p t h -> p (t h)").unsqueeze(2).to_broadcast(
                                            [P, HALF * H, D]),
                                        ALU.mult).then_inc(hv_ready, 1)

            def finish(k, w, b):
                dve.wait_ge(z_ready, k + 1)
                nc.vector.tensor_tensor(z[:, :, :], z_ps[:, b, 0:HALF, :],
                                        bo_sb[:, None, :].to_broadcast([P, HALF, F]), ALU.add).then_inc(z_step, 1)
                dve.wait_ge(z_step, k + 1)
                nc.vector.scalar_tensor_tensor(out=y[:, :, :], in0=z[:, :, :], scalar=SLOPE, in1=z[:, :, :],
                                               op0=ALU.mult, op1=ALU.max).then_inc(y_step, 1)
                dve.wait_ge(y_step, k + 1)
                need(dve, res_out[b], 16 * w)
                nc.vector.tensor_tensor(res[:, b, :, :], y[:, :, :], xs[:, b, :, :], ALU.add).then_inc(res_ready, 1)

            hand_over(0, 0)
            hand_over(1, 1)
            scores(0, 0, 0)
            hand_over(2, 0)
            scores(1, 0, 1)
            hand_over(3, 1)
            finish(0, 0, 0)
            with dve.Fori(1, NSTEP // 2 - 1) as w:
                scores(2 * w, w, 0)
                hand_over(2 * w + 2, 0)
                finish(2 * w - 1, w - 1, 1)
                scores(2 * w + 1, w, 1)
                hand_over(2 * w + 3, 1)
                finish(2 * w, w, 0)
            scores(NSTEP - 2, NSTEP // 2 - 1, 0)
            finish(NSTEP - 3, NSTEP // 2 - 2, 1)
            scores(NSTEP - 1, NSTEP // 2 - 1, 1)
            finish(NSTEP - 2, NSTEP // 2 - 1, 0)
            finish(NSTEP - 1, NSTEP // 2 - 1, 1)


def kernel(**inputs):
    import numpy as np
    import concourse.bacc as bacc
    from concourse.bass_utils import run_bass_kernel_spmd

    def padded(a, rows, value):
        tail = np.full((rows - a.shape[0],) + a.shape[1:], value, a.dtype)
        return np.concatenate([a, tail])

    g = {k: np.asarray(v) for k, v in inputs.items()}
    src = padded(g["src"], EPAD, 0)
    dst = padded(g["dst"], EPAD, N)
    before = np.concatenate([np.full(1, -1, dst.dtype), dst[:-1]])

    def by_tile(a):
        return a.reshape(NSUP, SUP, NCH, P).transpose(2, 0, 3, 1).reshape(NCH * NSUP, P, SUP)

    ea = padded(g["edge_attr_128"], EPAD, 0).reshape(NSUP, SUP, NCH, P, F).transpose(2, 0, 4, 1, 3)
    arrays = {
        "x": padded(g["x"], NPAD, 0),
        "idx": np.concatenate([by_tile(src), by_tile(dst)], axis=2),
        "dst_rows": dst.reshape(P * NCH, P),
        "dst_prev": before.reshape(P, T),
        "dst_first": dst[::P].reshape(1, NCH * P),
        "ea": ea.reshape(NCH * NSUP, F, SUP * P),
        "dist": padded(g["edge_weight1"], EPAD, 1).reshape(P, T),
        "wqvT": np.concatenate([g["L0_gnn_Wq"].T, g["L0_gnn_Wv"].T], axis=1),
        "bqv": np.concatenate([g["L0_gnn_bq"], g["L0_gnn_bv"]]).reshape(1, 2 * F),
        "wkT": g["L0_gnn_Wk"].T,
        "bk": g["L0_gnn_bk"].reshape(1, F),
        "woT": g["L0_gnn_Wo"].T,
        "bo": g["L0_gnn_bo"].reshape(1, F),
        "lam": g["L0_gnn_lam"].reshape(1, 1),
        "ident": np.eye(P, dtype=np.float32),
        "iota": np.concatenate([np.arange(P)[:, None] * NT + np.arange(-1, NT)[None, :],
                                np.arange(P)[:, None] * T - 1], axis=1).astype(np.float32),
    }
    nc = bacc.Bacc("TRN2", target_bir_lowering=False, num_devices=1)
    feeds, args = {}, []
    for name, a in arrays.items():
        a = np.ascontiguousarray(a)
        feeds[f"in_{name}"] = a
        args.append(nc.dram_tensor(f"in_{name}", a.shape, mybir.dt.from_np(a.dtype), kind="ExternalInput").ap())
    args.append(nc.dram_tensor("out_0", (NPAD, F), F32, kind="ExternalOutput").ap())
    gnn_kernel(nc, *args)
    r = run_bass_kernel_spmd(nc, [feeds], core_ids=[0])
    return r.results[0]["out_0"][:N]
```

```python
from contextlib import ExitStack

import concourse.bass as bass
from concourse import mybir

ALU = mybir.AluOpType
ACT = mybir.ActivationFunctionType
AX_X = mybir.AxisListType.X
F32 = mybir.dt.float32
I32 = mybir.dt.int32
BF16 = mybir.dt.bfloat16

P = 128
N, E, F = 12500, 212500, 128
H, D = 8, 16
SCALE = 1.0 / D ** 0.5
EPS = 1e-5
SLOPE = 0.1
NT = -(-N // P)
NPAD = P * NT
HALF = NT // 14
NSTEP = NT // HALF
NCH = -(-E // (P * P))
T = NCH * P
EPAD = P * T
SUP = 16
NSUP = P // SUP
GRP = 4
NG = SUP // GRP
CH = 3 * H
CPS = CH // NSUP
W1 = P + 1
ROW = 3 * CH
BIG = 1e30
NN = NT + 1
NCOL = NCH * NSUP
LB = 11
NB = NN // LB
TINY = 2.0 ** -63
assert NCOL >= NN and NB * LB == NN and NB % 2


def need(eng, sem, n):
    if not isinstance(n, int) or n > 0:
        eng.wait_ge(sem, n)


def gnn_kernel(nc, x, idx, dst_rows, dst_prev, dst_first, ea, dist, wqvT, bqv, wkT, bk, woT, bo, lam, ident_in,
               iota_in, square_in, out):
    q_tab = nc.dram_tensor("q_tab", (NPAD + P, F), F32, kind="Internal").ap()
    near_tab = nc.dram_tensor("near_tab", (3, EPAD), BF16, kind="Internal").ap()
    v_tab = nc.dram_tensor("v_tab", (NPAD, F), F32, kind="Internal").ap()
    state = nc.dram_tensor("state", (EPAD, ROW), F32, kind="Internal").ap()
    x_v = x.rearrange("(p t) f -> p (t f)", p=P)
    q_v = q_tab[0:NPAD, :].rearrange("(p t) f -> p (t f)", p=P)
    v_v = v_tab.rearrange("(p t) f -> p (t f)", p=P)
    out_v = out.rearrange("(p t) f -> p (t f)", p=P)
    state_v = state.rearrange("(p t) r -> p (t r)", p=P)

    with ExitStack() as ctx:
        def sb(name, shape, dt=F32):
            return ctx.enter_context(nc.sbuf_tensor(name, shape, dt))

        def sem(name):
            return ctx.enter_context(nc.semaphore(name))

        ident = sb("ident", [P, P])
        wk_sb = sb("wk_sb", [P, F])
        bk3_sb = sb("bk3_sb", [3, GRP * F], BF16)
        ones3_sb = sb("ones3_sb", [3, P], BF16)
        square_sb = sb("square_sb", [5, P], BF16)
        bases = sb("bases", [1, T], I32)
        first_f = sb("first_f", [P, T])
        nid = sb("nid", [P, NCOL + 1])
        nidh = sb("nidh", [P, NCOL])
        pen = sb("pen", [P, T])
        att = sb("att", [P, T])
        last_i = sb("last_i", [P, NT + 1], I32)
        has = sb("has", [P, NT])
        fix_i = sb("fix_i", [P, 1], I32)
        whole_pen = sb("whole_pen", [P, 1])
        cont_pen = sb("cont_pen", [P, 1])

        node_pass(nc, locals())
        rows = sb("rows", [P, P, ROW])
        edge_pass(nc, locals(), rows)
        finish_runs(nc, locals(), rows)

        out_pass(nc, locals())


def node_pass(nc, env):
    ident, wk_sb, bk3_sb, ones3_sb, square_sb, bases, first_f, nid, nidh = (env[k] for k in (
        "ident", "wk_sb", "bk3_sb", "ones3_sb", "square_sb", "bases", "first_f", "nid", "nidh"))
    pen, att, fix_i, whole_pen, cont_pen = (env[k] for k in ("pen", "att", "fix_i", "whole_pen", "cont_pen"))
    x_v, q_v, v_v, q_tab, dst_rows, dst_prev, dst_first, near_tab = (env[k] for k in (
        "x_v", "q_v", "v_v", "q_tab", "dst_rows", "dst_prev", "dst_first", "near_tab"))
    NLOAD = 9
    with ExitStack() as ctx:
        def sb(name, shape, dt=F32):
            return ctx.enter_context(nc.sbuf_tensor(name, shape, dt))

        def psum(name, shape):
            return ctx.enter_context(nc.psum_tensor(name, shape, F32))

        def sem(name):
            return ctx.enter_context(nc.semaphore(name))

        xs = sb("xs", [P, 2, HALF, F])
        stats = sb("stats", [P, 2, HALF, 6])
        mv = sb("mv", [P, 2, HALF, 2])
        sd = sb("sd", [P, 2, HALF])
        rstd = sb("rstd", [P, 2, HALF])
        nmr = sb("nmr", [P, 2, HALF])
        hb = sb("hb", [P, 2, HALF, F])
        hT = sb("hT", [P, 2, HALF, P])
        qs = sb("qs", [P, 2, HALF, F])
        vs = sb("vs", [P, 2, HALF, F])
        hT_ps = psum("hT_ps", [P, 8, P])
        qv_ps = psum("qv_ps", [P, 8, 2 * F])

        dst_i = sb("dst_i", [P, 2, T], I32)
        dst_f = sb("dst_f", [P, T])
        prev_f = sb("prev_f", [P, T])
        same = sb("same", [P, T])
        first_i = sb("first_i", [P, T], I32)
        dist_sb = sb("dist_sb", [P, T])
        lnd = sb("lnd", [P, T])
        clipped = sb("clipped", [P, T])
        power = sb("power", [P, T])
        keep = sb("keep", [P, T])
        lam0 = sb("lam0", [P, 1])
        lam_sb = sb("lam_sb", [P, 1])
        eps_sb = sb("eps_sb", [P, 1])
        wqv_sb = sb("wqv_sb", [P, 2 * F])
        bqv_sb = sb("bqv_sb", [P, 2 * F])
        bk_f = sb("bk_f", [1, F])
        bk_left = sb("bk_left", [1, 2, F])
        bk_parts = sb("bk_parts", [1, 3, F], BF16)
        zeros = sb("zeros", [P, F])
        rel = sb("rel", [P, T])
        rel2 = sb("rel2", [P, T])
        rel2_i = sb("rel2_i", [P, T], I32)
        high_i = sb("high_i", [P, T], I32)
        low_i = sb("low_i", [P, T], I32)
        near = sb("near", [P, 3, T], BF16)
        nfirst = sb("nfirst", [P, 4])

        consts = sem("consts")
        dve_turns = sem("dve_turns")
        made = sem("made")
        x_in = [sem("x_in0"), sem("x_in1")]
        stat_step = sem("stat_step")
        mv_ready = sem("mv_ready")
        sd_ready = sem("sd_ready")
        rstd_ready = sem("rstd_ready")
        nmr_ready = sem("nmr_ready")
        h_ready = sem("h_ready")
        hT_ready = sem("hT_ready")
        hT_copied = sem("hT_copied")
        qv_ready = sem("qv_ready")
        qv_copied = sem("qv_copied")
        q_out = [sem("q_out0"), sem("q_out1")]
        dst_in = sem("dst_in")
        first_in = sem("first_in")
        step = sem("step")
        ln_ready = sem("ln_ready")
        power_ready = sem("power_ready")
        clipped_ready = sem("clipped_ready")
        bk_ready = sem("bk_ready")
        bk_out = sem("bk_out")
        near_ready = sem("near_ready")
        near_out = sem("near_out")
        zeros_ready = sem("zeros_ready")

        block = ctx.enter_context(nc.Block())

        @block.sync
        def _(sp):
            sp.dma_start(dst_i[:, 0, :], dst_rows.rearrange("(p c) i -> p (c i)", p=P)).then_inc(dst_in, 16)
            sp.dma_start(dst_i[:, 1, :], dst_prev).then_inc(dst_in, 16)
            sp.dma_start(first_i[:, :], dst_first.to_broadcast([P, T])).then_inc(first_in, 16)
            sp.dma_start(bases[:, :], dst_first).then_inc(first_in, 16)
            sp.dma_start(ident[:, :], env["ident_in"]).then_inc(consts, 16)
            sp.dma_start(nid[:, :], env["iota_in"]).then_inc(consts, 16)
            sp.dma_start(wqv_sb[:, :], env["wqvT"]).then_inc(consts, 16)
            sp.dma_start(bqv_sb[:, :], env["bqv"].to_broadcast([P, 2 * F])).then_inc(consts, 16)
            sp.dma_start(wk_sb[:, :], env["wkT"]).then_inc(consts, 16)
            sp.dma_start(bk_f[:, :], env["bk"]).then_inc(consts, 16)
            sp.dma_start(square_sb[:, :], env["square_in"]).then_inc(consts, 16)
            sp.dma_start(lam_sb[:, :], env["lam"].to_broadcast([P, 1])).then_inc(consts, 16)
            sp.dma_start(dist_sb[:, :], env["dist"]).then_inc(consts, 16)

            def step_pair(w):
                for b in range(2):
                    k = 2 * w + b
                    need(sp, h_ready, k - 1)
                    sp.dma_start(xs[:, b, :, :], x_v[:, bass.ds(k * HALF * F, HALF * F)]).then_inc(x_in[b], 16)

            def store_pair(w):
                for b in range(2):
                    k = 2 * w + b
                    sp.wait_ge(qv_copied, k + 1)
                    sp.dma_start(q_v[:, bass.ds(k * HALF * F, HALF * F)], qs[:, b, :, :]).then_inc(q_out[b], 16)
                    sp.dma_start(v_v[:, bass.ds(k * HALF * F, HALF * F)], vs[:, b, :, :]).then_inc(q_out[b], 16)

            step_pair(0)
            with sp.Fori(1, NSTEP // 2) as w:
                step_pair(w)
                store_pair(w - 1)
            store_pair(NSTEP // 2 - 1)
            sp.wait_ge(bk_ready, 1)
            for j in range(3):
                for g in range(GRP):
                    sp.dma_start(bk3_sb[j:j + 1, g * F:(g + 1) * F], bk_parts[:, j, :]).then_inc(bk_out, 16)
            sp.wait_ge(zeros_ready, 1)
            sp.dma_start(q_tab[NPAD:NPAD + P, :], zeros[:, :]).then_inc(bk_out, 16)
            sp.wait_ge(near_ready, 3)
            for j in range(3):
                sp.dma_start(near_tab[j:j + 1, :].rearrange("o (p t) -> (o p) t", p=P), near[:, j, :]
                             ).then_inc(near_out, 16)
            sp.wait_ge(near_out, 48)
            sp.wait_ge(bk_out, 16 * (3 * GRP + 1))
            for b in range(2):
                sp.wait_ge(q_out[b], 32 * (NSTEP // 2))
            sp.wait_ge(consts, 16 * NLOAD)

        @block.scalar
        def _(act):
            def node_step(k, b):
                act.wait_ge(mv_ready, k + 1)
                nc.scalar.activation(sd[:, b, :], mv[:, b, :, 1], ACT.Sqrt, bias=eps_sb[:, 0:1]).then_inc(sd_ready, 1)
                act.wait_ge(nmr_ready, k + 1)
                for j in range(HALF):
                    h = nc.scalar.activation(hb[:, b, j, :], xs[:, b, j, :], ACT.Relu, bias=nmr[:, b, j:j + 1],
                                             scale=rstd[:, b, j:j + 1])
                h.then_inc(h_ready, 1)
                act.wait_ge(hT_ready, k + 1)
                nc.scalar.copy(hT[:, b, :, :], hT_ps[:, 0:HALF, :]).then_inc(hT_copied, 1)

            act.wait_ge(made, 2)
            with act.Fori(0, NSTEP // 2) as w:
                for b in range(2):
                    node_step(2 * w + b, b)
            act.wait_ge(clipped_ready, 1)
            nc.scalar.activation(lnd[:, :], clipped[:, :], ACT.Ln).then_inc(ln_ready, 1)
            act.wait_ge(ln_ready, 1)
            nc.scalar.activation(power[:, :], lnd[:, :], ACT.Exp, scale=lam_sb[:, 0:1]).then_inc(power_ready, 1)

        @block.tensor
        def _(pe):
            def node_step(k, b):
                pe.wait_ge(h_ready, k + 1)
                need(pe, hT_copied, k)
                for j in range(HALF):
                    t = nc.tensor.transpose(hT_ps[:, j, :], hb[:, b, j, :], ident[:, :])
                t.then_inc(hT_ready, 1)
                pe.wait_ge(hT_copied, k + 1)
                need(pe, qv_copied, k)
                for j in range(HALF):
                    m = nc.tensor.matmul(qv_ps[:, j, :], hT[:, b, j, :], wqv_sb[:, :], start=True, stop=True)
                m.then_inc(qv_ready, 1)

            pe.wait_ge(consts, 16 * NLOAD)
            node_step(0, 0)
            node_step(1, 1)
            with pe.Fori(1, NSTEP // 2) as w:
                for b in range(2):
                    node_step(2 * w + b, b)

        @block.vector
        def _(dve):
            nc.vector.memset(eps_sb[:, :], EPS).then_inc(made, 1)
            nc.vector.memset(ones3_sb[:, :], 1.0).then_inc(made, 1)
            nc.vector.memset(zeros[:, :], 0.0).then_inc(zeros_ready, 1)

            def normalise(k, b):
                dve.wait_ge(sd_ready, k + 1)
                nc.vector.reciprocal(rstd[:, b, :], sd[:, b, :]).then_inc(rstd_ready, 1)
                dve.wait_ge(rstd_ready, k + 1)
                nc.vector.scalar_tensor_tensor(out=nmr[:, b, :], in0=mv[:, b, :, 0], scalar=-1.0, in1=rstd[:, b, :],
                                               op0=ALU.mult, op1=ALU.mult).then_inc(nmr_ready, 1)

            def node_stats(k, w, b):
                dve.wait_ge(x_in[b], 16 * (w + 1))
                for j in range(HALF):
                    s = nc.vector.bn_stats(stats[:, b, j, :], xs[:, b, j, :])
                s.then_inc(stat_step, 1)
                dve.wait_ge(stat_step, k + 1)
                dve.sem_inc(dve_turns, 1)
                for j in range(HALF):
                    a = nc.vector.bn_aggr(mv[:, b, j, :], stats[:, b, j, :])
                a.then_inc(mv_ready, 1)

            def take_qv(k, w, b):
                dve.wait_ge(qv_ready, k + 1)
                need(dve, q_out[b], 32 * w)
                for o, c0 in ((qs, 0), (vs, F)):
                    c = nc.vector.tensor_tensor(o[:, b, :, :], qv_ps[:, 0:HALF, c0:c0 + F],
                                                bqv_sb[:, None, c0:c0 + F].to_broadcast([P, HALF, F]), ALU.add)
                c.then_inc(qv_copied, 1)

            def pair(w):
                for b in range(2):
                    k = 2 * w + b
                    node_stats(k, w, b)
                    normalise(k, b)
                    take_qv(k, w, b)

            dve.wait_ge(first_in, 32)
            nc.vector.tensor_copy(first_f[:, :], first_i[:, :]).then_inc(step, 1)
            dve.wait_ge(consts, 16 * NLOAD)
            nc.vector.tensor_scalar(nidh[:, :], nid[:, 0:NCOL], 0.5, None, ALU.add).then_inc(step, 1)
            dve.wait_ge(dst_in, 32)
            nc.vector.tensor_copy(dst_f[:, :], dst_i[:, 0, :]).then_inc(step, 1)
            nc.vector.tensor_copy(prev_f[:, :], dst_i[:, 1, :]).then_inc(step, 1)
            dve.wait_ge(step, 4)
            nc.vector.tensor_scalar(clipped[:, :], dist_sb[:, :], TINY, None, ALU.max).then_inc(clipped_ready, 1)
            nc.vector.tensor_scalar(lam0[:, :], lam_sb[:, :], 0.0, None, ALU.is_le).then_inc(step, 1)
            nc.vector.tensor_tensor(same[:, :], dst_f[:, :], prev_f[:, :], ALU.is_equal).then_inc(step, 1)
            dve.wait_ge(step, 6)
            nc.vector.tensor_scalar(pen[:, :], same[:, :], -1.0, BIG, ALU.add, ALU.mult).then_inc(step, 1)
            nc.vector.tensor_copy(nfirst[:, 1:2], dst_f[:, 0:1]).then_inc(step, 1)
            dve.wait_ge(step, 8)
            nc.vector.tensor_tensor(prev_f[:, :], dst_f[:, :], nfirst[:, 1:2].to_broadcast([P, T]), ALU.is_equal
                                    ).then_inc(step, 1)
            dve.wait_ge(step, 9)
            nc.vector.tensor_reduce(nfirst[:, 0:1], prev_f[:, :], AX_X, ALU.add).then_inc(step, 1)
            nc.vector.tensor_copy(cont_pen[:, :], pen[:, 0:1]).then_inc(step, 1)
            dve.wait_ge(step, 11)
            nc.vector.tensor_scalar(nfirst[:, 2:3], nfirst[:, 0:1], float(T), -1.0, ALU.is_equal, ALU.add
                                    ).then_inc(step, 1)
            dve.wait_ge(step, 12)
            nc.vector.scalar_tensor_tensor(out=whole_pen[:, :], in0=nfirst[:, 2:3], scalar=BIG, in1=cont_pen[:, :],
                                           op0=ALU.mult, op1=ALU.add).then_inc(step, 1)
            nc.vector.tensor_tensor(nfirst[:, 3:4], nfirst[:, 0:1], nid[:, NCOL:NCOL + 1], ALU.add).then_inc(step, 1)
            dve.wait_ge(step, 14)
            nc.vector.tensor_copy(fix_i[:, :], nfirst[:, 3:4]).then_inc(step, 1)

            pair(0)
            with dve.Fori(1, NSTEP // 2) as w:
                pair(w)

            nc.vector.tensor_copy(bk_parts[:, 0, :], bk_f[:, :]).then_inc(step, 1)
            dve.wait_ge(step, 16)
            nc.vector.tensor_tensor(bk_left[:, 0, :], bk_f[:, :], bk_parts[:, 0, :], ALU.subtract).then_inc(step, 1)
            dve.wait_ge(step, 17)
            nc.vector.tensor_copy(bk_parts[:, 1, :], bk_left[:, 0, :]).then_inc(step, 1)
            dve.wait_ge(step, 18)
            nc.vector.tensor_tensor(bk_left[:, 1, :], bk_left[:, 0, :], bk_parts[:, 1, :], ALU.subtract
                                    ).then_inc(step, 1)
            dve.wait_ge(step, 19)
            nc.vector.tensor_copy(bk_parts[:, 2, :], bk_left[:, 1, :]).then_inc(bk_ready, 1)
            nc.vector.tensor_tensor(rel[:, :].rearrange("p (c i) -> p c i", i=P),
                                    dst_f[:, :].rearrange("p (c i) -> p c i", i=P),
                                    dst_f[:, ::P].unsqueeze(2).to_broadcast([P, NCH, P]), ALU.subtract
                                    ).then_inc(step, 1)
            dve.wait_ge(step, 20)
            nc.vector.tensor_copy(near[:, 2, :], rel[:, :]).then_inc(near_ready, 1)
            nc.vector.tensor_tensor(rel2[:, :], rel[:, :], rel[:, :], ALU.mult).then_inc(step, 1)
            dve.wait_ge(step, 21)
            nc.vector.tensor_copy(rel2_i[:, :], rel2[:, :]).then_inc(step, 1)
            dve.wait_ge(step, 22)
            nc.vector.tensor_scalar(high_i[:, :], rel2_i[:, :], 0x7FFFFF00, None, ALU.bitwise_and).then_inc(step, 1)
            nc.vector.tensor_scalar(low_i[:, :], rel2_i[:, :], 0xFF, None, ALU.bitwise_and).then_inc(step, 1)
            dve.wait_ge(step, 24)
            nc.vector.tensor_copy(near[:, 0, :], high_i[:, :]).then_inc(near_ready, 1)
            nc.vector.tensor_copy(near[:, 1, :], low_i[:, :]).then_inc(near_ready, 1)
            nc.vector.tensor_scalar(keep[:, :], dist_sb[:, :], TINY, lam0[:, 0:1], ALU.is_ge, ALU.max
                                    ).then_inc(step, 1)
            dve.wait_ge(step, 25)
            dve.wait_ge(power_ready, 1)
            nc.vector.tensor_tensor(att[:, :], power[:, :], keep[:, :], ALU.mult).then_inc(step, 1)


def edge_pass(nc, env, rows):
    ident, wk_sb, bk3_sb, ones3_sb, square_sb, bases, first_f, nid, nidh = (env[k] for k in (
        "ident", "wk_sb", "bk3_sb", "ones3_sb", "square_sb", "bases", "first_f", "nid", "nidh"))
    pen, att, last_i, has = (env[k] for k in ("pen", "att", "last_i", "has"))
    q_tab, idx, ea, state_v, near_tab, dst_rows = (env[k] for k in (
        "q_tab", "idx", "ea", "state_v", "near_tab", "dst_rows"))
    near_v = near_tab.rearrange("j (p t) -> j p t", p=P)
    with ExitStack() as ctx:
        def sb(name, shape, dt=F32):
            return ctx.enter_context(nc.sbuf_tensor(name, shape, dt))

        def psum(name, shape):
            return ctx.enter_context(nc.psum_tensor(name, shape, F32))

        def sem(name):
            return ctx.enter_context(nc.semaphore(name))

        ea_sb = sb("ea_sb", [P, 2, SUP * P])
        idx_sb = sb("idx_sb", [P, 2, SUP], I32)
        near_sb = sb("near_sb", [5, 2, SUP * P], BF16)
        window = sb("window", [P, NG, GRP, F])
        onehot = sb("onehot", [P, 2, GRP * P])
        qpair = sb("qpair", [P, NG, 2, GRP * F])
        prod = sb("prod", [P, 2, 3, GRP * F])
        logits = sb("logits", [P, 2, CH, P])
        staged = sb("staged", [P, CPS, P])
        pen3 = sb("pen3", [P, CPS, W1])
        terms = sb("terms", [P, 4, CPS, W1])
        sums = sb("sums", [P, 3, CPS, W1])
        diffs = sb("diffs", [P, 2, CPS, P])
        shifted = sb("shifted", [P, CPS, P])
        sign_out = sb("sign_out", [P, T], BF16)
        signs = sb("signs", [P, NCOL])
        tile_f = sb("tile_f", [P, NN])
        tile_i = sb("tile_i", [P, NN], I32)
        tile_b = sb("tile_b", [P, 2, LB], I32)
        cnt = sb("cnt", [P, NN])
        last_f = sb("last_f", [P, NN])
        rows_i = ea_sb[:, :, 0:LB * P].bitcast(I32)
        k_ps = psum("k_ps", [P, 2, GRP * F])
        qd_ps = psum("qd_ps", [P, 2, GRP * F])
        sq_ps = psum("sq_ps", [P, 2, GRP * P])
        t_ps = psum("t_ps", [P, 4, P])

        ea_in = [sem("ea_in0"), sem("ea_in1")]
        idx_in = [sem("idx_in0"), sem("idx_in1")]
        near_in = [sem("near_in0"), sem("near_in1")]
        q_in = [sem(f"q_in{g}") for g in range(NG)]
        window_in = [sem(f"window_in{g}") for g in range(NG)]
        squares_ready = sem("squares_ready")
        onehot_ready = sem("onehot_ready")
        k_ready = sem("k_ready")
        qd_ready = sem("qd_ready")
        qd_copied = sem("qd_copied")
        prods_ready = sem("prods_ready")
        logits_ready = sem("logits_ready")
        staged_ready = sem("staged_ready")
        turned = sem("turned")
        terms_ready = sem("terms_ready")
        max_ready = sem("max_ready")
        shift_ready = sem("shift_ready")
        diffs_ready = sem("diffs_ready")
        exps_ready = sem("exps_ready")
        weighted_ready = sem("weighted_ready")
        sums_ready = sem("sums_ready")
        rows_ready = sem("rows_ready")
        rows_out = sem("rows_out")
        ones_ready = sem("ones_ready")
        pool_turns = sem("pool_turns1")
        signs_ready = sem("signs_ready")
        step = sem("tile_step")
        batch_ready = sem("batch_ready")
        rows_in = [sem("rows_in0"), sem("rows_in1")]
        rows_used = sem("rows_used")
        le_ready = sem("le_ready")

        block = ctx.enter_context(nc.Block())

        def over_chunks(eng, pair):
            pair(0, 0)
            with eng.Fori(1, NSUP // 2) as h:
                pair(0, h)
            with eng.Fori(1, NCH) as c:
                with eng.Fori(0, NSUP // 2) as h:
                    pair(c, h)

        @block.sync
        def _(sp):
            def pair(c, h):
                for b in range(2):
                    u = c * NSUP + 2 * h + b
                    need(sp, prods_ready, NG * (u - 1))
                    sp.dma_start(idx_sb[:, b, :], idx[bass.ds(u, 1), :, :].rearrange("a p n -> (a p) n")
                                 ).then_inc(idx_in[b], 16)
                    sp.dma_start(near_sb[0:3, b, :].rearrange("j (r i) -> j r i", r=SUP),
                                 near_v[:, bass.ds((2 * h + b) * SUP, SUP), bass.ds(c * P, P)]
                                 ).then_inc(near_in[b], 16)
                    sp.dma_start(ea_sb[:, b, :], ea[bass.ds(u, 1), :, :].rearrange("a p n -> (a p) n")
                                 ).then_inc(ea_in[b], 16)
                    for g in range(NG):
                        _, base = nc.values_load_multi_w_load_instructions(
                            bases[0:1, bass.ds(u * SUP + g * GRP, GRP)], engines=(mybir.EngineType.SP,),
                            min_val=0, max_val=N, skip_runtime_bounds_check_because="dst is a node's number")
                        need(sp, prods_ready, NG * (u - 1) + g + 1)
                        for j in range(GRP):
                            sp.dma_start(window[:, g, j, :], q_tab[bass.ds(base[j], P), :]
                                         ).then_inc(window_in[g], 16)

            sp.wait_ge(ones_ready, 1)
            over_chunks(sp, pair)

        @block.gpsimd
        def _(pool):
            def pair(c, h):
                for b in range(2):
                    w = c * (NSUP // 2) + h
                    u = 2 * w + b
                    pool.wait_ge(idx_in[b], 16 * (w + 1))
                    for g in range(NG):
                        need(pool, prods_ready, NG * (u - 1) + g + 1)
                        pool.sem_inc(pool_turns, 1)
                        for j in range(GRP):
                            pool.indirect_dma_start(
                                out=qpair[:, g, 0, j * F:(j + 1) * F], out_offset=None, in_=q_tab,
                                in_offset=bass.IndirectOffsetOnAxis(
                                    ap=idx_sb[:, b, g * GRP + j:g * GRP + j + 1], axis=0)
                            ).then_inc(q_in[g], 16)

            over_chunks(pool, pair)

            def batch(m, b):
                pool.wait_ge(batch_ready, m + 1)
                pool.sem_inc(pool_turns, 1)
                for j in range(LB):
                    pool.indirect_dma_start(out=rows_i[:, b, j * P:(j + 1) * P], out_offset=None, in_=dst_rows,
                                            in_offset=bass.IndirectOffsetOnAxis(ap=tile_b[:, b, j:j + 1], axis=0)
                                            ).then_inc(rows_in[b], 16)

            with pool.Fori(0, NB // 2) as m:
                batch(2 * m, 0)
                batch(2 * m + 1, 1)
            batch(NB - 1, 0)

        @block.tensor
        def _(pe):
            def squares(n, w, b, g):
                if g == 0:
                    pe.wait_ge(near_in[b], 16 * (w + 1))
                need(pe, onehot_ready, n - 1)
                nc.tensor.matmul(sq_ps[:, g % 2, :], square_sb[:, :], near_sb[:, b, g * GRP * P:(g + 1) * GRP * P],
                                 start=True, stop=True).then_inc(squares_ready, 1)

            def keys(n, w, b, g):
                if g == 0:
                    pe.wait_ge(ea_in[b], 16 * (w + 1))
                need(pe, prods_ready, n - 1)
                nc.tensor.matmul(k_ps[:, g % 2, :], ones3_sb[:, :], bk3_sb[:, :], start=True, stop=False,
                                 skip_group_check=True)
                for j in range(GRP):
                    t = g * GRP + j
                    m = nc.tensor.matmul(k_ps[:, g % 2, j * F:(j + 1) * F], ea_sb[:, b, t * P:(t + 1) * P],
                                         wk_sb[:, :], start=False, stop=True, skip_group_check=True)
                m.then_inc(k_ready, 1)

            def pick(n, u, g):
                pe.wait_ge(window_in[g], 16 * GRP * (u + 1))
                need(pe, qd_copied, n - 1)
                pe.wait_ge(onehot_ready, n + 1)
                for j in range(GRP):
                    m = nc.tensor.matmul(qd_ps[:, g % 2, j * F:(j + 1) * F], onehot[:, g % 2, j * P:(j + 1) * P],
                                         window[:, g, j, :], start=True, stop=True)
                m.then_inc(qd_ready, 1)

            def turn(c, h, b):
                v = (c - 1) * NSUP + 2 * h + b
                pe.wait_ge(staged_ready, v + 1)
                for j in range(CPS):
                    t = nc.tensor.transpose(t_ps[:, j, :], staged[:, j, :], ident[:, :])
                t.then_inc(turned, 1)

            def pair(c, h):
                for b in range(2):
                    w = c * (NSUP // 2) + h
                    u = 2 * w + b
                    n = NG * u
                    squares(n, w, b, 0)
                    for g in range(NG):
                        if g + 1 < NG:
                            squares(n + g + 1, w, b, g + 1)
                        keys(n + g, w, b, g)
                        pick(n + g, u, g)
                        if g == 0 and (not isinstance(c, int) or c > 0):
                            turn(c, h, b)

            over_chunks(pe, pair)
            with pe.Fori(0, NSUP // 2) as h:
                for b in range(2):
                    turn(NCH, h, b)

        @block.scalar
        def _(act):
            def pick_mask(n, g):
                act.wait_ge(squares_ready, n + 1)
                need(act, qd_ready, n - 1)
                nc.scalar.activation(onehot[:, g % 2, :], sq_ps[:, g % 2, :], ACT.Relu, bias=1.0, scale=-1.0
                                     ).then_inc(onehot_ready, 1)

            def take_qd(n, u, g):
                act.wait_ge(qd_ready, n + 1)
                need(act, prods_ready, n - NG + 1)
                nc.scalar.copy(qpair[:, g, 1, :], qd_ps[:, g % 2, :]).then_inc(qd_copied, 1)

            def count_tiles(u):
                need(act, signs_ready, u)
                nc.scalar.activation(sign_out[:, :], first_f[:, :], ACT.Sign, bias=nidh[:, bass.ds(u, 1)],
                                     scale=-1.0, accum_out=signs[:, bass.ds(u, 1)]).then_inc(signs_ready, 1)

            def stage(c, s, v):
                act.wait_ge(logits_ready, NG * NSUP * c)
                nc.scalar.copy(staged[:, :, :],
                               logits[:, bass.ds((c - 1) % 2, 1), bass.ds(s * CPS, CPS), :].rearrange(
                                   "p a c i -> p (a c) i")).then_inc(staged_ready, 1)
                nc.scalar.copy(pen3[:, :, 1:W1],
                               pen[:, None, bass.ds((c - 1) * P, P)].to_broadcast([P, CPS, P]))
                act.wait_ge(rows_ready, v + 1)
                nc.scalar.copy(terms[:, 1:4, :, 0:1].rearrange("p k c o -> p k (c o)"),
                               rows[:, P - 1, :].rearrange("p (k c) -> p k c", k=3)[:, :, bass.ds(s * CPS, CPS)])

            def take_turned(v):
                act.wait_ge(turned, v + 1)
                nc.scalar.copy(terms[:, 1, :, 1:W1], t_ps[:, 0:CPS, :]).then_inc(terms_ready, 1)

            def exps(v):
                act.wait_ge(diffs_ready, v + 1)
                nc.scalar.activation(terms[:, 0:3:2, :, 1:W1], diffs[:, :, :, :], ACT.Exp, scale=SCALE
                                     ).then_inc(exps_ready, 1)

            def take_sums(c, s, v):
                act.wait_ge(sums_ready, v + 1)
                need(act, rows_out, 16 * (c - 1))
                nc.scalar.copy(
                    rows[:, :, :].rearrange("p i (k c) -> p k c i", k=3)[:, :, bass.ds(s * CPS, CPS), :],
                    sums[:, :, :, 1:W1]).then_inc(rows_ready, 1)

            def pair(c, h):
                scans = not isinstance(c, int) or c > 0
                for b in range(2):
                    s = 2 * h + b
                    u = c * NSUP + s
                    v = u - NSUP
                    n = NG * u
                    pick_mask(n, 0)
                    pick_mask(n + 1, 1)
                    if scans:
                        stage(c, s, v)
                    take_qd(n, u, 0)
                    if scans:
                        take_turned(v)
                    pick_mask(n + 2, 2)
                    take_qd(n + 1, u, 1)
                    if scans:
                        exps(v)
                    pick_mask(n + 3, 3)
                    take_qd(n + 2, u, 2)
                    count_tiles(u)
                    take_qd(n + 3, u, 3)
                    if scans:
                        take_sums(c, s, v)

            def store(c):
                act.wait_ge(rows_ready, NSUP * c + 1)
                act.dma_start(state_v[:, bass.ds((c - 1) * P * ROW, P * ROW)],
                              rows[:, :, :].rearrange("p i r -> p (i r)")).then_inc(rows_out, 16)

            act.wait_ge(ones_ready, 3)
            pair(0, 0)
            with act.Fori(1, NSUP // 2) as h:
                pair(0, h)
            with act.Fori(0, NSUP // 2) as h:
                pair(1, h)
            store(1)
            with act.Fori(2, NCH) as c:
                with act.Fori(0, NSUP // 2) as h:
                    pair(c, h)
                store(c)
            with act.Fori(0, NSUP // 2) as h:
                for b in range(2):
                    s = 2 * h + b
                    v = (NCH - 1) * NSUP + s
                    stage(NCH, s, v)
                    take_turned(v)
                    exps(v)
                    take_sums(NCH, s, v)
            store(NCH)
            act.wait_ge(rows_out, 16 * NCH)

        @block.vector
        def _(dve):
            nc.vector.memset(near_sb[:, :, :], 1.0).then_inc(ones_ready, 1)
            nc.vector.memset(rows[:, P - 1, 0:CH], -BIG)
            nc.vector.memset(rows[:, P - 1, CH:ROW], 0.0).then_inc(rows_ready, 1)
            nc.vector.memset(pen3[:, :, 0:1], -BIG).then_inc(ones_ready, 1)
            nc.vector.memset(terms[:, 0, :, 0:1], 0.0).then_inc(ones_ready, 1)

            def edges(c, h, b, g):
                u = c * NSUP + 2 * h + b
                n = NG * u + g
                dve.wait_ge(q_in[g], 16 * GRP * (u + 1))
                need(dve, logits_ready, n - 1)
                dve.wait_ge(k_ready, n + 1)
                dve.wait_ge(qd_copied, n + 1)
                nc.vector.tensor_tensor(prod[:, g % 2, 0:2, :],
                                        k_ps[:, g % 2, :].unsqueeze(1).to_broadcast([P, 2, GRP * F]),
                                        qpair[:, g, :, :], ALU.mult)
                nc.vector.tensor_tensor(prod[:, g % 2, 2, :], qpair[:, g, 0, :], qpair[:, g, 1, :], ALU.mult
                                        ).then_inc(prods_ready, 1)
                dve.wait_ge(prods_ready, n + 1)
                for a in range(3):
                    o = logits[:, bass.ds(c % 2, 1), a * H:(a + 1) * H,
                               bass.ds((2 * h + b) * SUP + g * GRP, GRP)].rearrange("p a c r -> p r (a c)")
                    r = nc.vector.tensor_reduce(o, prod[:, g % 2, a, :].rearrange("p (r c d) -> p r c d", r=GRP,
                                                                                  d=D), AX_X, ALU.add)
                r.then_inc(logits_ready, 1)

            def running_max(c, h, b):
                v = (c - 1) * NSUP + 2 * h + b
                dve.wait_ge(rows_ready, v + 1)
                dve.wait_ge(terms_ready, v + 1)
                nc.vector.tensor_tensor_scan(sums[:, 0, :, :].rearrange("p c i -> p (c i)"),
                                             pen3[:, :, :].rearrange("p c i -> p (c i)"),
                                             terms[:, 1, :, :].rearrange("p c i -> p (c i)"), -BIG, ALU.add, ALU.max
                                             ).then_inc(max_ready, 1)
                dve.wait_ge(max_ready, v + 1)
                nc.vector.tensor_tensor(shifted[:, :, :], sums[:, 0, :, 0:P], pen3[:, :, 1:W1], ALU.add
                                        ).then_inc(shift_ready, 1)
                nc.vector.tensor_tensor(diffs[:, 1, :, :], terms[:, 1, :, 1:W1], sums[:, 0, :, 1:W1], ALU.subtract)
                dve.wait_ge(shift_ready, v + 1)
                nc.vector.tensor_tensor(diffs[:, 0, :, :], shifted[:, :, :], sums[:, 0, :, 1:W1], ALU.subtract
                                        ).then_inc(diffs_ready, 1)

            def running_sums(c, h, b):
                v = (c - 1) * NSUP + 2 * h + b
                dve.wait_ge(exps_ready, v + 1)
                nc.vector.tensor_tensor(terms[:, 3, :, 1:W1], terms[:, 2, :, 1:W1],
                                        att[:, None, bass.ds((c - 1) * P, P)].to_broadcast([P, CPS, P]), ALU.mult
                                        ).then_inc(weighted_ready, 1)
                dve.wait_ge(weighted_ready, v + 1)
                for k in (1, 2):
                    s = nc.vector.tensor_tensor_scan(sums[:, k, :, :].rearrange("p c i -> p (c i)"),
                                                     terms[:, 0, :, :].rearrange("p c i -> p (c i)"),
                                                     terms[:, k + 1, :, :].rearrange("p c i -> p (c i)"), 0.0,
                                                     ALU.mult, ALU.add)
                s.then_inc(sums_ready, 1)

            def pair(c, h):
                scans = not isinstance(c, int) or c > 0
                for b in range(2):
                    edges(c, h, b, 0)
                    if scans:
                        running_max(c, h, b)
                    edges(c, h, b, 1)
                    edges(c, h, b, 2)
                    if scans:
                        running_sums(c, h, b)
                    edges(c, h, b, 3)

            over_chunks(dve, pair)

            dve.wait_ge(signs_ready, NCOL)
            nc.vector.tensor_scalar(last_f[:, :], signs[:, 0:NN], 0.5, T // 2 - 1.0, ALU.mult, ALU.add
                                    ).then_inc(step, 1)
            dve.wait_ge(step, 1)
            nc.vector.tensor_scalar(tile_f[:, :], last_f[:, :], 0.0, None, ALU.max).then_inc(step, 1)
            dve.wait_ge(step, 2)
            nc.vector.tensor_copy(tile_i[:, :], tile_f[:, :]).then_inc(step, 1)
            dve.wait_ge(step, 3)

            def hand_over(m, b):
                nc.vector.tensor_copy(tile_b[:, b, :], tile_i[:, bass.ds(m * LB, LB)]).then_inc(batch_ready, 1)

            hand_over(0, 0)
            hand_over(1, 1)
            with dve.Fori(0, NSUP // 2) as h:
                for b in range(2):
                    running_max(NCH, h, b)
                    running_sums(NCH, h, b)

            le = prod[:, 0, 0:3, :].rearrange("p a n -> p (a n)")[:, 0:LB * P].rearrange("p (l i) -> p l i", i=P)

            def count(m, b, done):
                dve.wait_ge(rows_in[b], done)
                need(dve, rows_used, m)
                nc.vector.tensor_tensor(le, rows_i[:, b, :].rearrange("p (l i) -> p l i", i=P),
                                        nid[:, bass.ds(m * LB, LB)].unsqueeze(2).to_broadcast([P, LB, P]), ALU.is_le
                                        ).then_inc(le_ready, 1)
                dve.wait_ge(le_ready, m + 1)
                nc.vector.tensor_reduce(cnt[:, bass.ds(m * LB, LB)], le, AX_X, ALU.add).then_inc(rows_used, 1)

            def two_counts(m):
                for b in range(2):
                    count(2 * m + b, b, 16 * LB * (m + 1))
                    hand_over(2 * m + b + 2, b)

            dve.wait_ge(logits_ready, NG * NCOL)
            two_counts(0)
            with dve.Fori(1, NB // 2 - 1) as m:
                two_counts(m)
            count(NB - 3, 0, 16 * LB * (NB // 2))
            hand_over(NB - 1, 0)
            count(NB - 2, 1, 16 * LB * (NB // 2))
            count(NB - 1, 0, 16 * LB * (NB // 2 + 1))
            dve.wait_ge(rows_used, NB)
            nc.vector.scalar_tensor_tensor(out=last_f[:, :], in0=tile_f[:, :], scalar=float(P), in1=cnt[:, :],
                                           op0=ALU.mult, op1=ALU.add).then_inc(step, 1)
            dve.wait_ge(step, 4)
            nc.vector.tensor_tensor(has[:, :], last_f[:, 1:NN], last_f[:, 0:NT], ALU.is_gt)
            nc.vector.tensor_scalar(last_i[:, :], last_f[:, :], -1.0, 0.0, ALU.add, ALU.max).then_inc(step, 1)


def finish_runs(nc, env, rows):
    ident, fix_i, whole_pen, cont_pen, state = (env[k] for k in (
        "ident", "fix_i", "whole_pen", "cont_pen", "state"))
    with ExitStack() as ctx:
        def sb(name, shape, dt=F32):
            return ctx.enter_context(nc.sbuf_tensor(name, shape, dt))

        def psum(name, shape):
            return ctx.enter_context(nc.psum_tensor(name, shape, F32))

        def sem(name):
            return ctx.enter_context(nc.semaphore(name))

        pens = sb("pens", [P, 2, CH])
        ends = sb("ends", [CH, 5, P])
        open_ = sb("open_", [CH, 3, W1])
        diff = sb("diff", [CH, 2, P])
        fac = sb("fac", [CH, 2, P])
        scaled = sb("scaled", [CH, 2, P])
        carry_t = sb("carry_t", [CH, 3, P])
        carry = sb("carry", [P, 3, CH])
        fix = sb("fix", [P, 3, CH])
        best = sb("best", [P, CH])
        cdiff = sb("cdiff", [P, 2, CH])
        cfac = sb("cfac", [P, 2, CH])
        part = sb("part", [P, 2, 2, CH])
        fixed = sb("fixed", [P, 3, CH])
        ends_ps = psum("ends_ps", [P, 2, 4, P])
        carry_ps = psum("carry_ps", [P, 4, P])

        fix_in = sem("fix_in")
        fix_out = sem("fix_out")
        pens_ready = sem("pens_ready")
        ends_turned = sem("ends_turned")
        dve_step = sem("dve_step")
        diff_ready = sem("diff_ready")
        fac_ready = sem("fac_ready")
        carry_ready = sem("carry_ready")
        carry_turned = sem("carry_turned")
        cdiff_ready = sem("cdiff_ready")
        cfac_ready = sem("cfac_ready")
        fixed_ready = sem("fixed_ready")
        block = ctx.enter_context(nc.Block())

        @block.gpsimd
        def _(pool):
            pool.indirect_dma_start(out=fix[:, :, :].rearrange("p k c -> p (k c)"), out_offset=None, in_=state,
                                    in_offset=bass.IndirectOffsetOnAxis(ap=fix_i[:, 0:1], axis=0)
                                    ).then_inc(fix_in, 16)
            pool.wait_ge(fixed_ready, 1)
            pool.indirect_dma_start(out=state, out_offset=bass.IndirectOffsetOnAxis(ap=fix_i[:, 0:1], axis=0),
                                    in_=fixed[:, :, :].rearrange("p k c -> p (k c)"), in_offset=None
                                    ).then_inc(fix_out, 16)
            pool.wait_ge(fix_out, 16)

        @block.tensor
        def _(pe):
            for k in range(3):
                nc.tensor.transpose(ends_ps[0:CH, 0, k, :], rows[:, P - 1, k * CH:(k + 1) * CH], ident[:, :])
            pe.wait_ge(pens_ready, 2)
            nc.tensor.transpose(ends_ps[0:CH, 1, 0, :], pens[:, 0, :], ident[:, :])
            nc.tensor.transpose(ends_ps[0:CH, 1, 1, :], pens[:, 1, :], ident[:, :]).then_inc(ends_turned, 1)
            pe.wait_ge(carry_ready, 3)
            for k in range(3):
                t = nc.tensor.transpose(carry_ps[:, k, 0:CH], carry_t[:, k, :], ident[0:CH, 0:CH])
            t.then_inc(carry_turned, 1)

        @block.scalar
        def _(act):
            act.wait_ge(diff_ready, 1)
            nc.scalar.activation(fac[:, :, :], diff[:, :, :], ACT.Exp, scale=SCALE).then_inc(fac_ready, 1)
            act.wait_ge(cdiff_ready, 1)
            nc.scalar.activation(cfac[:, :, :], cdiff[:, :, :], ACT.Exp, scale=SCALE).then_inc(cfac_ready, 1)

        @block.vector
        def _(dve):
            nc.vector.tensor_copy(pens[:, 0, :], whole_pen[:, 0:1].to_broadcast([P, CH])).then_inc(pens_ready, 1)
            nc.vector.tensor_copy(pens[:, 1, :], cont_pen[:, 0:1].to_broadcast([P, CH])).then_inc(pens_ready, 1)
            nc.vector.memset(open_[:, 0, 0:1], -BIG)
            nc.vector.memset(open_[:, 1:3, 0:1], 0.0)
            dve.wait_ge(ends_turned, 1)
            nc.vector.tensor_copy(ends[:, 0:3, :], ends_ps[0:CH, 0, 0:3, :])
            nc.vector.tensor_copy(ends[:, 3:5, :], ends_ps[0:CH, 1, 0:2, :]).then_inc(dve_step, 1)
            dve.wait_ge(dve_step, 1)
            nc.vector.tensor_tensor_scan(open_[:, 0, 1:W1], ends[:, 3, :], ends[:, 0, :], -BIG, ALU.add, ALU.max
                                         ).then_inc(dve_step, 1)
            dve.wait_ge(dve_step, 2)
            nc.vector.tensor_tensor(diff[:, 0, :], open_[:, 0, 0:P], ends[:, 3, :], ALU.add).then_inc(dve_step, 1)
            nc.vector.tensor_tensor(diff[:, 1, :], ends[:, 0, :], open_[:, 0, 1:W1], ALU.subtract)
            dve.wait_ge(dve_step, 3)
            nc.vector.tensor_tensor(diff[:, 0, :], diff[:, 0, :], open_[:, 0, 1:W1], ALU.subtract
                                    ).then_inc(diff_ready, 1)
            dve.wait_ge(fac_ready, 1)
            for k in range(2):
                m = nc.vector.tensor_tensor(scaled[:, k, :], ends[:, 1 + k, :], fac[:, 1, :], ALU.mult)
            m.then_inc(dve_step, 1)
            dve.wait_ge(dve_step, 4)
            for k in range(2):
                m = nc.vector.tensor_tensor_scan(open_[:, 1 + k, 1:W1], fac[:, 0, :], scaled[:, k, :], 0.0, ALU.mult,
                                                 ALU.add)
            m.then_inc(dve_step, 1)
            dve.wait_ge(dve_step, 5)
            nc.vector.tensor_tensor(carry_t[:, 0, :], open_[:, 0, 0:P], ends[:, 4, :], ALU.add
                                    ).then_inc(carry_ready, 1)
            for k in (1, 2):
                nc.vector.tensor_copy(carry_t[:, k, :], open_[:, k, 0:P]).then_inc(carry_ready, 1)
            dve.wait_ge(carry_turned, 1)
            nc.vector.tensor_copy(carry[:, :, :], carry_ps[:, 0:3, 0:CH]).then_inc(dve_step, 1)
            dve.wait_ge(dve_step, 6)
            dve.wait_ge(fix_in, 16)
            nc.vector.tensor_tensor(best[:, :], carry[:, 0, :], fix[:, 0, :], ALU.max).then_inc(dve_step, 1)
            dve.wait_ge(dve_step, 7)
            nc.vector.tensor_tensor(cdiff[:, 0, :], carry[:, 0, :], best[:, :], ALU.subtract)
            nc.vector.tensor_tensor(cdiff[:, 1, :], fix[:, 0, :], best[:, :], ALU.subtract).then_inc(cdiff_ready, 1)
            dve.wait_ge(cfac_ready, 1)
            for k in range(2):
                nc.vector.tensor_tensor(part[:, k, 0, :], carry[:, 1 + k, :], cfac[:, 0, :], ALU.mult)
                m = nc.vector.tensor_tensor(part[:, k, 1, :], fix[:, 1 + k, :], cfac[:, 1, :], ALU.mult)
            m.then_inc(dve_step, 1)
            dve.wait_ge(dve_step, 8)
            nc.vector.tensor_copy(fixed[:, 0, :], best[:, :])
            nc.vector.tensor_tensor(fixed[:, 1:3, :], part[:, :, 0, :], part[:, :, 1, :], ALU.add
                                    ).then_inc(fixed_ready, 1)


def out_pass(nc, env):
    ident, last_i, has, state, x_v, v_v, out_v = (env[k] for k in (
        "ident", "last_i", "has", "state", "x_v", "v_v", "out_v"))
    with ExitStack() as ctx:
        def sb(name, shape, dt=F32):
            return ctx.enter_context(nc.sbuf_tensor(name, shape, dt))

        def psum(name, shape):
            return ctx.enter_context(nc.psum_tensor(name, shape, F32))

        def sem(name):
            return ctx.enter_context(nc.semaphore(name))

        wo_sb = sb("wo_sb", [P, F])
        bo_sb = sb("bo_sb", [P, F])
        xs = sb("xs2", [P, 2, HALF, F])
        vs = sb("vs2", [P, 2, HALF, F])
        last_b = sb("last_b", [P, 2, HALF], I32)
        st = sb("st", [P, 2, HALF, 3, CH])
        rden = sb("rden", [P, HALF, CH])
        ratio = sb("ratio", [P, HALF, CH])
        score = sb("score", [P, HALF, H])
        score_m = sb("score_m", [P, HALF, H])
        hv = sb("hv", [P, 2, HALF, F])
        hvT = sb("hvT", [P, 2, HALF, P])
        z = sb("z", [P, HALF, F])
        y = sb("y", [P, HALF, F])
        res = sb("res", [P, 2, HALF, F])
        hT_ps = psum("hT_ps2", [P, 2, 8, P])
        z_ps = psum("z_ps", [P, 2, 8, P])

        wo_in = sem("wo_in")
        in_sem = [sem("in0"), sem("in1")]
        batch_ready = sem("batch_ready2")
        pool_turns = sem("pool_turns2")
        st_in = [sem("st_in0"), sem("st_in1")]
        step = [sem(f"node_step{i}") for i in range(4)]
        hv_ready = sem("hv_ready")
        hvT_ready = sem("hvT_ready")
        hvT_copied = sem("hvT_copied")
        z_ready = sem("z_ready")
        z_step = sem("z_step")
        y_step = sem("y_step")
        res_ready = sem("res_ready")
        res_out = [sem("res_out0"), sem("res_out1")]
        block = ctx.enter_context(nc.Block())

        @block.sync
        def _(sp):
            def load(w):
                for b in range(2):
                    k = 2 * w + b
                    need(sp, res_ready, k - 1)
                    sp.dma_start(xs[:, b, :, :], x_v[:, bass.ds(k * HALF * F, HALF * F)]).then_inc(in_sem[b], 16)
                    sp.dma_start(vs[:, b, :, :], v_v[:, bass.ds(k * HALF * F, HALF * F)]).then_inc(in_sem[b], 16)

            sp.dma_start(wo_sb[:, :], env["woT"]).then_inc(wo_in, 16)
            sp.dma_start(bo_sb[:, :], env["bo"].to_broadcast([P, F])).then_inc(wo_in, 16)
            load(0)
            with sp.Fori(1, NSTEP // 2) as w:
                load(w)

        @block.gpsimd
        def _(pool):
            with pool.Fori(0, NSTEP // 2) as w:
                for b in range(2):
                    pool.wait_ge(batch_ready, 2 * w + b + 1)
                    pool.sem_inc(pool_turns, 1)
                    for j in range(HALF):
                        pool.indirect_dma_start(out=st[:, b, j, :, :].rearrange("p k c -> p (k c)"), out_offset=None,
                                                in_=state,
                                                in_offset=bass.IndirectOffsetOnAxis(ap=last_b[:, b, j:j + 1], axis=0)
                                                ).then_inc(st_in[b], 16)

        @block.tensor
        def _(pe):
            def turn(k, b):
                pe.wait_ge(hv_ready, k + 1)
                for j in range(HALF):
                    t = nc.tensor.transpose(hT_ps[:, b, j, :], hv[:, b, j, :], ident[:, :])
                t.then_inc(hvT_ready, 1)

            def project(k, b):
                pe.wait_ge(hvT_copied, k + 1)
                need(pe, z_step, k - 1)
                for j in range(HALF):
                    m = nc.tensor.matmul(z_ps[:, b, j, :], hvT[:, b, j, :], wo_sb[:, :], start=True, stop=True)
                m.then_inc(z_ready, 1)

            pe.wait_ge(wo_in, 32)
            turn(0, 0)
            project(0, 0)
            turn(1, 1)
            project(1, 1)
            with pe.Fori(1, NSTEP // 2) as w:
                for b in range(2):
                    turn(2 * w + b, b)
                    project(2 * w + b, b)

        @block.scalar
        def _(act):
            def copy(k, b):
                act.wait_ge(hvT_ready, k + 1)
                nc.scalar.copy(hvT[:, b, :, :], hT_ps[:, b, 0:HALF, :]).then_inc(hvT_copied, 1)

            def store(k, b):
                act.wait_ge(res_ready, k + 1)
                act.dma_start(out_v[:, bass.ds(k * HALF * F, HALF * F)], res[:, b, :, :]).then_inc(res_out[b], 16)

            copy(0, 0)
            copy(1, 1)
            store(0, 0)
            with act.Fori(1, NSTEP // 2) as w:
                copy(2 * w, 0)
                store(2 * w - 1, 1)
                copy(2 * w + 1, 1)
                store(2 * w, 0)
            store(NSTEP - 1, 1)
            for b in range(2):
                act.wait_ge(res_out[b], 16 * (NSTEP // 2))

        @block.vector
        def _(dve):
            def hand_over(k, b):
                nc.vector.tensor_copy(last_b[:, b, :], last_i[:, bass.ds(k * HALF + 1, HALF)]
                                      ).then_inc(batch_ready, 1)

            def scores(k, w, b):
                dve.wait_ge(st_in[b], 16 * HALF * (w + 1))
                nc.vector.reciprocal(rden[:, :, :], st[:, b, :, 1, :]).then_inc(step[0], 1)
                dve.wait_ge(step[0], k + 1)
                nc.vector.tensor_tensor(ratio[:, :, :], st[:, b, :, 2, :], rden[:, :, :], ALU.mult
                                        ).then_inc(step[1], 1)
                dve.wait_ge(step[1], k + 1)
                nc.vector.tensor_reduce(score[:, :, :], ratio[:, :, :].rearrange("p t (a h) -> p t h a", a=3), AX_X,
                                        ALU.add).then_inc(step[2], 1)
                dve.wait_ge(step[2], k + 1)
                nc.vector.tensor_tensor(score_m[:, :, :], score[:, :, :],
                                        has[:, bass.ds(k * HALF, HALF)].unsqueeze(2).to_broadcast([P, HALF, H]),
                                        ALU.mult).then_inc(step[3], 1)
                dve.wait_ge(step[3], k + 1)
                dve.wait_ge(in_sem[b], 32 * (w + 1))
                nc.vector.tensor_tensor(hv[:, b, :, :].rearrange("p t (h d) -> p (t h) d", h=H),
                                        vs[:, b, :, :].rearrange("p t (h d) -> p (t h) d", h=H),
                                        score_m[:, :, :].rearrange("p t h -> p (t h)").unsqueeze(2).to_broadcast(
                                            [P, HALF * H, D]),
                                        ALU.mult).then_inc(hv_ready, 1)

            def finish(k, w, b):
                dve.wait_ge(z_ready, k + 1)
                nc.vector.tensor_tensor(z[:, :, :], z_ps[:, b, 0:HALF, :],
                                        bo_sb[:, None, :].to_broadcast([P, HALF, F]), ALU.add).then_inc(z_step, 1)
                dve.wait_ge(z_step, k + 1)
                nc.vector.scalar_tensor_tensor(out=y[:, :, :], in0=z[:, :, :], scalar=SLOPE, in1=z[:, :, :],
                                               op0=ALU.mult, op1=ALU.max).then_inc(y_step, 1)
                dve.wait_ge(y_step, k + 1)
                need(dve, res_out[b], 16 * w)
                nc.vector.tensor_tensor(res[:, b, :, :], y[:, :, :], xs[:, b, :, :], ALU.add).then_inc(res_ready, 1)

            dve.wait_ge(wo_in, 32)
            hand_over(0, 0)
            hand_over(1, 1)
            scores(0, 0, 0)
            hand_over(2, 0)
            scores(1, 0, 1)
            hand_over(3, 1)
            finish(0, 0, 0)
            with dve.Fori(1, NSTEP // 2 - 1) as w:
                scores(2 * w, w, 0)
                hand_over(2 * w + 2, 0)
                finish(2 * w - 1, w - 1, 1)
                scores(2 * w + 1, w, 1)
                hand_over(2 * w + 3, 1)
                finish(2 * w, w, 0)
            scores(NSTEP - 2, NSTEP // 2 - 1, 0)
            finish(NSTEP - 3, NSTEP // 2 - 2, 1)
            scores(NSTEP - 1, NSTEP // 2 - 1, 1)
            finish(NSTEP - 2, NSTEP // 2 - 1, 0)
            finish(NSTEP - 1, NSTEP // 2 - 1, 1)


def kernel(**inputs):
    import ml_dtypes
    import numpy as np
    import concourse.bacc as bacc
    from concourse.bass_utils import run_bass_kernel_spmd

    def padded(a, rows, value):
        tail = np.full((rows - a.shape[0],) + a.shape[1:], value, a.dtype)
        return np.concatenate([a, tail])

    g = {k: np.asarray(v) for k, v in inputs.items()}
    src = padded(g["src"], EPAD, 0)
    dst = padded(g["dst"], EPAD, N)
    before = np.concatenate([np.full(1, -1, dst.dtype), dst[:-1]])

    one, at = np.ones(P, np.int64), np.arange(P)

    def by_tile(a):
        return a.reshape(NSUP, SUP, NCH, P).transpose(2, 0, 3, 1).reshape(NCH * NSUP, P, SUP)

    ea = padded(g["edge_attr_128"], EPAD, 0).reshape(NSUP, SUP, NCH, P, F).transpose(2, 0, 4, 1, 3)
    arrays = {
        "x": padded(g["x"], NPAD, 0),
        "idx": by_tile(src),
        "dst_rows": dst.reshape(P * NCH, P),
        "dst_prev": before.reshape(P, T),
        "dst_first": dst[::P].reshape(P, NCH).T.reshape(1, NCH * P),
        "ea": ea.reshape(NCH * NSUP, F, SUP * P),
        "dist": padded(g["edge_weight1"], EPAD, 1).reshape(P, T),
        "wqvT": np.concatenate([g["L0_gnn_Wq"].T, g["L0_gnn_Wv"].T], axis=1),
        "bqv": np.concatenate([g["L0_gnn_bq"], g["L0_gnn_bv"]]).reshape(1, 2 * F),
        "wkT": g["L0_gnn_Wk"].T,
        "bk": g["L0_gnn_bk"].reshape(1, F),
        "woT": g["L0_gnn_Wo"].T,
        "bo": g["L0_gnn_bo"].reshape(1, F),
        "lam": g["L0_gnn_lam"].reshape(1, 1),
        "ident": np.eye(P, dtype=np.float32),
        "iota": np.concatenate([np.arange(P)[:, None] * NT + np.arange(-1, NCOL - 1)[None, :],
                                np.arange(P)[:, None] * T - 1], axis=1).astype(np.float32),
        "square": np.stack([one, one, -2 * one * at, at * at // 256 * 256, at * at % 256]).astype(ml_dtypes.bfloat16),
    }
    nc = bacc.Bacc("TRN2", target_bir_lowering=False, num_devices=1)
    feeds, args = {}, []
    for name, a in arrays.items():
        a = np.ascontiguousarray(a)
        feeds[f"in_{name}"] = a
        args.append(nc.dram_tensor(f"in_{name}", a.shape, mybir.dt.from_np(a.dtype), kind="ExternalInput").ap())
    args.append(nc.dram_tensor("out_0", (NPAD, F), F32, kind="ExternalOutput").ap())
    gnn_kernel(nc, *args)
    r = run_bass_kernel_spmd(nc, [feeds], core_ids=[0])
    return r.results[0]["out_0"][:N]
```

```python
from contextlib import ExitStack

import concourse.bass as bass
from concourse import mybir

ALU = mybir.AluOpType
ACT = mybir.ActivationFunctionType
AX_X = mybir.AxisListType.X
F32 = mybir.dt.float32
I32 = mybir.dt.int32
BF16 = mybir.dt.bfloat16

P = 128
N, E, F = 12500, 212500, 128
H, D = 8, 16
SCALE = 1.0 / D ** 0.5
EPS = 1e-5
SLOPE = 0.1
NT = -(-N // P)
NPAD = P * NT
HALF = NT // 14
NSTEP = NT // HALF
NCH = -(-E // (P * P))
T = NCH * P
EPAD = P * T
SUP = 16
NSUP = P // SUP
GRP = 4
NG = SUP // GRP
CH = 3 * H
CPS = CH // NSUP
W1 = P + 1
ROW = 3 * CH
BIG = 2.0 ** 100
NN = NT + 1
NCOL = NCH * NSUP
LB = 11
NB = NN // LB
TINY = 2.0 ** -63
assert NCOL >= NN and NB * LB == NN and NB % 2


def need(eng, sem, n):
    if not isinstance(n, int) or n > 0:
        eng.wait_ge(sem, n)


def gnn_kernel(nc, x, idx, dst_rows, dst_prev, dst_first, ea, dist, wqvT, bqv, wkT, bk, woT, bo, lam, ident_in,
               iota_in, square_in, out):
    q_tab = nc.dram_tensor("q_tab", (NPAD + P, F), F32, kind="Internal").ap()
    near_tab = nc.dram_tensor("near_tab", (5, EPAD), BF16, kind="Internal").ap()
    v_tab = nc.dram_tensor("v_tab", (NPAD, F), F32, kind="Internal").ap()
    state = nc.dram_tensor("state", (EPAD, ROW), F32, kind="Internal").ap()
    x_v = x.rearrange("(p t) f -> p (t f)", p=P)
    q_v = q_tab[0:NPAD, :].rearrange("(p t) f -> p (t f)", p=P)
    v_v = v_tab.rearrange("(p t) f -> p (t f)", p=P)
    out_v = out.rearrange("(p t) f -> p (t f)", p=P)
    state_v = state.rearrange("(p t) r -> p (t r)", p=P)

    with ExitStack() as ctx:
        def sb(name, shape, dt=F32):
            return ctx.enter_context(nc.sbuf_tensor(name, shape, dt))

        def sem(name):
            return ctx.enter_context(nc.semaphore(name))

        ident = sb("ident", [P, P])
        wk_sb = sb("wk_sb", [P, F])
        bk3_sb = sb("bk3_sb", [3, GRP * F], BF16)
        ones3_sb = sb("ones3_sb", [3, P], BF16)
        square_sb = sb("square_sb", [5, P], BF16)
        first_f = sb("first_f", [P, T])
        nid = sb("nid", [P, NCOL + 1])
        nidh = sb("nidh", [P, NCOL])
        pen = sb("pen", [P, T], BF16)
        att = sb("att", [P, T])
        last_i = sb("last_i", [P, NT + 1], I32)
        has = sb("has", [P, NT])
        fix_i = sb("fix_i", [P, 1], I32)
        whole_pen = sb("whole_pen", [P, 1])
        cont_pen = sb("cont_pen", [P, 1])

        node_pass(nc, locals())
        rows = sb("rows", [P, 2, P, ROW])
        edge_pass(nc, locals(), rows)
        out_pass(nc, locals())


def node_pass(nc, env):
    ident, wk_sb, bk3_sb, ones3_sb, square_sb, first_f, nid, nidh = (env[k] for k in (
        "ident", "wk_sb", "bk3_sb", "ones3_sb", "square_sb", "first_f", "nid", "nidh"))
    pen, att, fix_i, whole_pen, cont_pen = (env[k] for k in ("pen", "att", "fix_i", "whole_pen", "cont_pen"))
    x_v, q_v, v_v, q_tab, dst_rows, dst_prev, dst_first, near_tab = (env[k] for k in (
        "x_v", "q_v", "v_v", "q_tab", "dst_rows", "dst_prev", "dst_first", "near_tab"))
    NLOAD = 9
    PARTS = (range(0, HALF // 2 + 1), range(HALF // 2 + 1, HALF))
    with ExitStack() as ctx:
        def sb(name, shape, dt=F32):
            return ctx.enter_context(nc.sbuf_tensor(name, shape, dt))

        def psum(name, shape):
            return ctx.enter_context(nc.psum_tensor(name, shape, F32))

        def sem(name):
            return ctx.enter_context(nc.semaphore(name))

        xs = sb("xs", [P, NT, F])
        stats = sb("stats", [P, 2, HALF, 6])
        mv = sb("mv", [P, 2, HALF, 2])
        sd = sb("sd", [P, NT])
        rstd = sb("rstd", [P, NT])
        nmr = sb("nmr", [P, NT])
        hb = sb("hb", [P, 2, HALF, F])
        hT = sb("hT", [P, 2, HALF, P])
        qs = sb("qs", [P, 2, HALF, F])
        vs = sb("vs", [P, 2, HALF, F])
        hT_ps = psum("hT_ps", [P, 2, 8, P])
        qv_ps = psum("qv_ps", [P, 8, 2 * F])

        dst_i = sb("dst_i", [P, 2, T], I32)
        dst_f = sb("dst_f", [P, T])
        prev_f = sb("prev_f", [P, T])
        same = sb("same", [P, T])
        first_i = sb("first_i", [P, T], I32)
        dist_sb = sb("dist_sb", [P, T])
        clipped = sb("clipped", [P, T])
        power = sb("power", [P, T])
        keep = sb("keep", [P, T])
        lam0 = sb("lam0", [P, 1])
        lam_sb = sb("lam_sb", [P, 1])
        eps_sb = sb("eps_sb", [P, 1])
        wqv_sb = sb("wqv_sb", [P, 2 * F])
        bqv_sb = sb("bqv_sb", [P, 2 * F])
        bk_f = sb("bk_f", [1, F])
        bk_left = sb("bk_left", [1, 2, F])
        bk_parts = sb("bk_parts", [1, 3, F], BF16)
        zeros = sb("zeros", [P, F])
        rel = sb("rel", [P, T])
        rel2_i = sb("rel2_i", [P, T], I32)
        rel2 = power
        high_i, low_i = dst_i[:, 0, :], dst_i[:, 1, :]
        near = sb("near", [P, 5, T], BF16)
        nfirst = sb("nfirst", [P, 4])

        consts = sem("consts")
        dve_turns = sem("dve_turns")
        made = sem("made")
        x_in = [sem("x_in0"), sem("x_in1")]
        stat_step = sem("stat_step")
        mv_ready = sem("mv_ready")
        sd_ready = sem("sd_ready")
        rstd_ready = sem("rstd_ready")
        nmr_ready = sem("nmr_ready")
        h_ready = sem("h_ready")
        hT_ready = sem("hT_ready")
        hT_copied = sem("hT_copied")
        qv_ready = sem("qv_ready")
        qv_copied = sem("qv_copied")
        q_out = [sem("q_out0"), sem("q_out1")]
        dst_in = sem("dst_in")
        first_in = sem("first_in")
        step = sem("step")
        pool_step = sem("pool_step")
        pool_made = sem("pool_made")
        parts_ready = sem("parts_ready")
        ln_ready = sem("ln_ready")
        power_ready = sem("power_ready")
        clipped_ready = sem("clipped_ready")
        bk_ready = sem("bk_ready")
        bk_out = sem("bk_out")
        near_ready = sem("near_ready")
        near_out = sem("near_out")
        zeros_ready = sem("zeros_ready")

        block = ctx.enter_context(nc.Block())

        @block.sync
        def _(sp):
            def load(k, b):
                need(sp, stat_step, k - 1)
                sp.dma_start(xs[:, bass.ds(k * HALF, HALF), :].rearrange("p t f -> p (t f)"),
                             x_v[:, bass.ds(k * HALF * F, HALF * F)]).then_inc(x_in[b], 16)

            def store(k, b):
                sp.wait_ge(qv_copied, 2 * k + 2)
                sp.dma_start(q_v[:, bass.ds(k * HALF * F, HALF * F)], qs[:, b, :, :]).then_inc(q_out[b], 16)
                sp.dma_start(v_v[:, bass.ds(k * HALF * F, HALF * F)], vs[:, b, :, :]).then_inc(q_out[b], 16)

            load(0, 0)
            load(1, 1)
            sp.dma_start(ident[:, :], env["ident_in"]).then_inc(consts, 16)
            sp.dma_start(nid[:, :], env["iota_in"]).then_inc(consts, 16)
            sp.dma_start(wqv_sb[:, :], env["wqvT"]).then_inc(consts, 16)
            sp.dma_start(bqv_sb[:, :], env["bqv"].to_broadcast([P, 2 * F])).then_inc(consts, 16)
            sp.dma_start(wk_sb[:, :], env["wkT"]).then_inc(consts, 16)
            sp.dma_start(bk_f[:, :], env["bk"]).then_inc(consts, 16)
            sp.dma_start(square_sb[:, :], env["square_in"]).then_inc(consts, 16)
            sp.dma_start(lam_sb[:, :], env["lam"].to_broadcast([P, 1])).then_inc(consts, 16)
            sp.dma_start(dist_sb[:, :], env["dist"]).then_inc(consts, 16)
            sp.dma_start(dst_i[:, 0, :], dst_rows.rearrange("(p c) i -> p (c i)", p=P)).then_inc(dst_in, 16)
            sp.dma_start(dst_i[:, 1, :], dst_prev).then_inc(dst_in, 16)
            sp.dma_start(first_i[:, :], dst_first[:, 0:T].to_broadcast([P, T])).then_inc(first_in, 16)
            load(2, 0)
            load(3, 1)
            sp.wait_ge(bk_ready, 1)
            for j in range(3):
                for g in range(GRP):
                    sp.dma_start(bk3_sb[j:j + 1, g * F:(g + 1) * F], bk_parts[:, j, :]).then_inc(bk_out, 16)
            load(4, 0)
            with sp.Fori(0, NSTEP // 2 - 3) as w:
                for b in range(2):
                    load(2 * w + 5 + b, 1 - b)
                    store(2 * w + b, b)
            load(NSTEP - 1, 1)
            for k in range(NSTEP - 6, NSTEP):
                store(k, k % 2)
            sp.wait_ge(zeros_ready, 1)
            sp.dma_start(q_tab[NPAD:NPAD + P, :], zeros[:, :]).then_inc(bk_out, 16)
            sp.wait_ge(near_ready, 4)
            for j in range(5):
                sp.dma_start(near_tab[j:j + 1, :].rearrange("o (p t) -> (o p) t", p=P), near[:, j, :]
                             ).then_inc(near_out, 16)
            sp.wait_ge(near_out, 16 * 5)
            sp.wait_ge(bk_out, 16 * (3 * GRP + 1))
            for b in range(2):
                sp.wait_ge(q_out[b], 32 * (NSTEP // 2))
            sp.wait_ge(consts, 16 * NLOAD)

        @block.scalar
        def _(act):
            def spread(k, b):
                act.wait_ge(mv_ready, k + 1)
                nc.scalar.activation(sd[:, bass.ds(k * HALF, HALF)], mv[:, b, :, 1], ACT.Sqrt,
                                     bias=eps_sb[:, 0:1]).then_inc(sd_ready, 1)

            def norm_relu(k, b):
                act.wait_ge(nmr_ready, k + 1)
                for j in range(HALF):
                    n = bass.ds(k * HALF + j, 1)
                    h = nc.scalar.activation(hb[:, b, j, :], xs[:, n, :].rearrange("p o f -> p (o f)"), ACT.Relu,
                                             bias=nmr[:, n], scale=rstd[:, n])
                h.then_inc(h_ready, 1)

            def copy_turned(k, b):
                act.wait_ge(hT_ready, k + 1)
                need(act, qv_ready, 2 * k - 2)
                nc.scalar.copy(hT[:, b, :, :], hT_ps[:, b, 0:HALF, :]).then_inc(hT_copied, 1)

            act.wait_ge(made, 2)
            spread(0, 0)
            spread(1, 1)
            norm_relu(0, 0)
            spread(2, 0)
            norm_relu(1, 1)
            copy_turned(0, 0)
            spread(3, 1)
            norm_relu(2, 0)
            with act.Fori(1, NSTEP // 2 - 1) as w:
                copy_turned(2 * w - 1, 1)
                spread(2 * w + 2, 0)
                norm_relu(2 * w + 1, 1)
                copy_turned(2 * w, 0)
                spread(2 * w + 3, 1)
                norm_relu(2 * w + 2, 0)
            copy_turned(NSTEP - 3, 1)
            norm_relu(NSTEP - 1, 1)
            copy_turned(NSTEP - 2, 0)
            copy_turned(NSTEP - 1, 1)
            act.wait_ge(clipped_ready, 1)
            act.wait_ge(near_ready, 4)
            nc.scalar.activation(clipped[:, :], clipped[:, :], ACT.Ln).then_inc(ln_ready, 1)
            act.wait_ge(ln_ready, 1)
            nc.scalar.activation(power[:, :], clipped[:, :], ACT.Exp, scale=lam_sb[:, 0:1]).then_inc(power_ready, 1)

        @block.tensor
        def _(pe):
            def turn(k, b):
                pe.wait_ge(h_ready, k + 1)
                need(pe, hT_copied, k - 1)
                for j in range(HALF):
                    t = nc.tensor.transpose(hT_ps[:, b, j, :], hb[:, b, j, :], ident[:, :])
                t.then_inc(hT_ready, 1)

            def project(k, b):
                pe.wait_ge(hT_copied, k + 1)
                for part, tiles in enumerate(PARTS):
                    need(pe, qv_copied, 2 * k - 1 + part)
                    for j in tiles:
                        m = nc.tensor.matmul(qv_ps[:, j, :], hT[:, b, j, :], wqv_sb[:, :], start=True, stop=True)
                    m.then_inc(qv_ready, 1)

            pe.wait_ge(consts, 16 * NLOAD)
            turn(0, 0)
            turn(1, 1)
            project(0, 0)
            with pe.Fori(1, NSTEP // 2) as w:
                turn(2 * w, 0)
                project(2 * w - 1, 1)
                turn(2 * w + 1, 1)
                project(2 * w, 0)
            project(NSTEP - 1, 1)

        @block.gpsimd
        def _(pool):
            nc.gpsimd.memset(near[:, 3:5, :], 1.0).then_inc(near_ready, 1)
            pool.wait_ge(dst_in, 32)
            nc.gpsimd.tensor_copy(dst_f[:, :], dst_i[:, 0, :]).then_inc(pool_step, 1)
            nc.gpsimd.tensor_copy(prev_f[:, :], dst_i[:, 1, :]).then_inc(pool_made, 1)
            pool.wait_ge(pool_step, 1)
            nc.gpsimd.tensor_tensor(rel[:, :].rearrange("p (c i) -> p c i", i=P),
                                    dst_f[:, :].rearrange("p (c i) -> p c i", i=P),
                                    dst_f[:, ::P].unsqueeze(2).to_broadcast([P, NCH, P]), ALU.subtract
                                    ).then_inc(pool_step, 1)
            pool.wait_ge(pool_step, 2)
            nc.gpsimd.tensor_copy(near[:, 2, :], rel[:, :]).then_inc(near_ready, 1)
            nc.gpsimd.tensor_tensor(rel2[:, :], rel[:, :], rel[:, :], ALU.mult).then_inc(pool_step, 1)
            pool.wait_ge(pool_step, 3)
            nc.gpsimd.tensor_copy(rel2_i[:, :], rel2[:, :]).then_inc(pool_made, 1)
            pool.wait_ge(first_in, 16)
            nc.gpsimd.tensor_copy(first_f[:, :], first_i[:, :]).then_inc(pool_made, 1)
            pool.wait_ge(parts_ready, 2)
            nc.gpsimd.tensor_copy(near[:, 0, :], high_i).then_inc(near_ready, 1)
            nc.gpsimd.tensor_copy(near[:, 1, :], low_i).then_inc(near_ready, 1)

        @block.vector
        def _(dve):
            nc.vector.memset(eps_sb[:, :], EPS).then_inc(made, 1)
            nc.vector.memset(ones3_sb[:, :], 1.0).then_inc(made, 1)
            nc.vector.memset(zeros[:, :], 0.0).then_inc(zeros_ready, 1)

            def normalise(k, b):
                dve.wait_ge(sd_ready, k + 1)
                n = bass.ds(k * HALF, HALF)
                nc.vector.reciprocal(rstd[:, n], sd[:, n]).then_inc(rstd_ready, 1)
                dve.wait_ge(rstd_ready, k + 1)
                nc.vector.scalar_tensor_tensor(out=nmr[:, n], in0=mv[:, b, :, 0], scalar=-1.0, in1=rstd[:, n],
                                               op0=ALU.mult, op1=ALU.mult).then_inc(nmr_ready, 1)

            def node_stats(k, w, b):
                dve.wait_ge(x_in[b], 16 * (w + 1))
                for j in range(HALF):
                    s = nc.vector.bn_stats(stats[:, b, j, :],
                                           xs[:, bass.ds(k * HALF + j, 1), :].rearrange("p o f -> p (o f)"))
                s.then_inc(stat_step, 1)
                dve.wait_ge(stat_step, k + 1)
                need(dve, nmr_ready, k - 1)
                dve.sem_inc(dve_turns, 1)
                for j in range(HALF):
                    a = nc.vector.bn_aggr(mv[:, b, j, :], stats[:, b, j, :])
                a.then_inc(mv_ready, 1)

            def take_qv(k, w, b):
                need(dve, q_out[b], 32 * w)
                for part, tiles in enumerate(PARTS):
                    dve.wait_ge(qv_ready, 2 * k + 1 + part)
                    j0, j1 = tiles[0], tiles[-1] + 1
                    for o, c0 in ((qs, 0), (vs, F)):
                        c = nc.vector.tensor_tensor(o[:, b, j0:j1, :], qv_ps[:, j0:j1, c0:c0 + F],
                                                    bqv_sb[:, None, c0:c0 + F].to_broadcast([P, j1 - j0, F]),
                                                    ALU.add)
                    c.then_inc(qv_copied, 1)

            def pair(w, ahead):
                for b in range(2):
                    k = 2 * w + b
                    if ahead > b:
                        node_stats(k + 3, w + 1 + b, 1 - b)
                    if ahead >= b:
                        normalise(k + 2, b)
                    take_qv(k, w, b)

            node_stats(0, 0, 0)
            node_stats(1, 0, 1)
            normalise(0, 0)
            node_stats(2, 1, 0)
            normalise(1, 1)
            dve.wait_ge(consts, 16 * NLOAD)
            nc.vector.tensor_copy(bk_parts[:, 0, :], bk_f[:, :]).then_inc(step, 1)
            nc.vector.tensor_scalar(nidh[:, :], nid[:, 0:NCOL], 0.5, None, ALU.add)
            dve.wait_ge(step, 1)
            nc.vector.tensor_tensor(bk_left[:, 0, :], bk_f[:, :], bk_parts[:, 0, :], ALU.subtract).then_inc(step, 1)
            nc.vector.tensor_scalar(lam0[:, :], lam_sb[:, :], 0.0, None, ALU.is_le).then_inc(step, 1)
            dve.wait_ge(step, 3)
            nc.vector.tensor_copy(bk_parts[:, 1, :], bk_left[:, 0, :]).then_inc(step, 1)
            dve.wait_ge(step, 4)
            nc.vector.tensor_tensor(bk_left[:, 1, :], bk_left[:, 0, :], bk_parts[:, 1, :], ALU.subtract
                                    ).then_inc(step, 1)
            dve.wait_ge(step, 5)
            nc.vector.tensor_copy(bk_parts[:, 2, :], bk_left[:, 1, :]).then_inc(bk_ready, 1)
            pair(0, 2)

            dve.wait_ge(pool_made, 1)
            nc.vector.tensor_tensor(same[:, :], dst_f[:, :], prev_f[:, :], ALU.is_equal).then_inc(step, 1)
            nc.vector.tensor_copy(nfirst[:, 1:2], dst_f[:, 0:1]).then_inc(step, 1)
            dve.wait_ge(step, 7)
            nc.vector.tensor_scalar(pen[:, :], same[:, :], -1.0, BIG, ALU.add, ALU.mult).then_inc(step, 1)
            nc.vector.tensor_tensor(prev_f[:, :], dst_f[:, :], nfirst[:, 1:2].to_broadcast([P, T]), ALU.is_equal
                                    ).then_inc(step, 1)
            dve.wait_ge(step, 9)
            nc.vector.tensor_reduce(nfirst[:, 0:1], prev_f[:, :], AX_X, ALU.add).then_inc(step, 1)
            nc.vector.tensor_copy(cont_pen[:, :], pen[:, 0:1]).then_inc(step, 1)
            dve.wait_ge(step, 11)
            nc.vector.tensor_scalar(nfirst[:, 2:3], nfirst[:, 0:1], float(T), -1.0, ALU.is_equal, ALU.add
                                    ).then_inc(step, 1)
            dve.wait_ge(step, 12)
            nc.vector.scalar_tensor_tensor(out=whole_pen[:, :], in0=nfirst[:, 2:3], scalar=BIG, in1=cont_pen[:, :],
                                           op0=ALU.mult, op1=ALU.add).then_inc(step, 1)
            nc.vector.tensor_tensor(nfirst[:, 3:4], nfirst[:, 0:1], nid[:, NCOL:NCOL + 1], ALU.add).then_inc(step, 1)
            dve.wait_ge(step, 14)
            nc.vector.tensor_copy(fix_i[:, :], nfirst[:, 3:4]).then_inc(step, 1)
            nc.vector.tensor_scalar(clipped[:, :], dist_sb[:, :], TINY, None, ALU.max).then_inc(clipped_ready, 1)
            nc.vector.tensor_scalar(keep[:, :], dist_sb[:, :], TINY, lam0[:, 0:1], ALU.is_ge, ALU.max
                                    ).then_inc(step, 1)
            dve.wait_ge(pool_made, 2)
            nc.vector.tensor_scalar(high_i, rel2_i[:, :], 0x7FFFFF00, None, ALU.bitwise_and).then_inc(parts_ready, 1)
            nc.vector.tensor_scalar(low_i, rel2_i[:, :], 0xFF, None, ALU.bitwise_and).then_inc(parts_ready, 1)

            with dve.Fori(1, NSTEP // 2 - 2) as w:
                pair(w, 2)
            pair(NSTEP // 2 - 2, 1)
            pair(NSTEP // 2 - 1, -1)
            dve.wait_ge(step, 16)
            dve.wait_ge(power_ready, 1)
            nc.vector.tensor_tensor(att[:, :], power[:, :], keep[:, :], ALU.mult)


def edge_pass(nc, env, rows):
    ident, wk_sb, bk3_sb, ones3_sb, square_sb, first_f, nid, nidh = (env[k] for k in (
        "ident", "wk_sb", "bk3_sb", "ones3_sb", "square_sb", "first_f", "nid", "nidh"))
    pen, att, last_i, has, fix_i, whole_pen, cont_pen, state = (env[k] for k in (
        "pen", "att", "last_i", "has", "fix_i", "whole_pen", "cont_pen", "state"))
    q_tab, idx, ea, state_v, near_tab, dst_rows = (env[k] for k in (
        "q_tab", "idx", "ea", "state_v", "near_tab", "dst_rows"))
    dst_first = env["dst_first"]
    near_v = near_tab.rearrange("j (p t) -> j p t", p=P)
    with ExitStack() as ctx:
        def sb(name, shape, dt=F32):
            return ctx.enter_context(nc.sbuf_tensor(name, shape, dt))

        def psum(name, shape):
            return ctx.enter_context(nc.psum_tensor(name, shape, F32))

        def sem(name):
            return ctx.enter_context(nc.semaphore(name))

        ea_sb = sb("ea_sb", [P, 2, SUP * P])
        bases = sb("bases", [1, 2, P], I32)
        idx_sb = sb("idx_sb", [P, 2, SUP], I32)
        near_sb = sb("near_sb", [5, 2, SUP * P], BF16)
        window = sb("window", [P, NG, GRP, F])
        onehot = sb("onehot", [P, 2, GRP * P])
        qpair = sb("qpair", [P, NG, 2, GRP * F])
        prod = sb("prod", [P, 2, 3, GRP * F])
        logits = sb("logits", [P, 2, CH, P])
        staged = sb("staged", [P, CPS, P])
        pen3 = sb("pen3", [P, CPS, W1])
        terms = sb("terms", [P, 4, CPS, W1])
        sums = sb("sums", [P, 3, CPS, W1])
        diffs = sb("diffs", [P, 2, CPS, P])
        shifted = sb("shifted", [P, CPS, P])
        sign_out = sb("sign_out", [P, T], BF16)
        signs = sb("signs", [P, NCOL])
        tile_f = sb("tile_f", [P, NN])
        tile_i = sb("tile_i", [P, NN], I32)
        tile_b = sb("tile_b", [P, 2, LB], I32)
        cnt = sb("cnt", [P, NN])
        last_f = sb("last_f", [P, NN])
        rows_i = ea_sb[:, :, 0:LB * P].bitcast(I32)
        flat = window[0:CH, :, :, :].rearrange("p g j f -> p (g j f)")

        def part_of(at, k, n):
            return flat[:, at:at + k * n].rearrange("p (k n) -> p k n", k=k)

        ends = part_of(0, 5, P)
        open_ = part_of(5 * P, 3, W1)
        diff, fac, scaled = (part_of(5 * P + 3 * W1 + 2 * P * k, 2, P) for k in range(3))
        carry_t = onehot[0:CH, 0, 0:3 * P].rearrange("p (k n) -> p k n", k=3)
        pens = sb("pens", [P, 2, CH])
        carry = sb("carry", [P, 3, CH])
        fix = sb("fix", [P, 3, CH])
        best = sb("best", [P, CH])
        cdiff = sb("cdiff", [P, 2, CH])
        cfac = sb("cfac", [P, 2, CH])
        part = sb("part", [P, 2, 2, CH])
        fixed = sb("fixed", [P, 3, CH])
        k_ps = psum("k_ps", [P, 2, GRP * F])
        qd_ps = psum("qd_ps", [P, 2, GRP * F])
        sq_ps = psum("sq_ps", [P, 2, GRP * P])
        t_ps = psum("t_ps", [P, 4, P])

        ea_in = [sem("ea_in0"), sem("ea_in1")]
        bases_in = sem("bases_in")
        idx_in = [sem("idx_in0"), sem("idx_in1")]
        near_in = [sem("near_in0"), sem("near_in1")]
        q_in = [sem(f"q_in{g}") for g in range(NG)]
        window_in = [sem(f"window_in{g}") for g in range(NG)]
        squares_ready = sem("squares_ready")
        onehot_ready = sem("onehot_ready")
        k_ready = sem("k_ready")
        qd_ready = sem("qd_ready")
        qd_copied = sem("qd_copied")
        prods_ready = sem("prods_ready")
        logits_ready = sem("logits_ready")
        staged_ready = sem("staged_ready")
        turned = sem("turned")
        terms_ready = sem("terms_ready")
        max_ready = sem("max_ready")
        shift_ready = sem("shift_ready")
        diffs_ready = sem("diffs_ready")
        exps_ready = sem("exps_ready")
        weighted_ready = sem("weighted_ready")
        sums_ready = sem("sums_ready")
        rows_ready = sem("rows_ready")
        rows_out = sem("rows_out")
        ones_ready = sem("ones_ready")
        pool_turns = sem("pool_turns1")
        signs_ready = sem("signs_ready")
        step = sem("tile_step")
        tiles_ready = sem("tiles_ready")
        tiles_copied = sem("tiles_copied")
        rows_in = [sem("rows_in0"), sem("rows_in1")]
        rows_used = sem("rows_used")
        le_ready = sem("le_ready")
        fix_in = sem("fix_in")
        fix_out = sem("fix_out")
        pens_ready = sem("pens_ready")
        ends_turned = sem("ends_turned")
        join_step = sem("join_step")
        diff_ready = sem("diff_ready")
        fac_ready = sem("fac_ready")
        carry_ready = sem("carry_ready")
        carry_turned = sem("carry_turned")
        cdiff_ready = sem("cdiff_ready")
        cfac_ready = sem("cfac_ready")
        fixed_ready = sem("fixed_ready")

        block = ctx.enter_context(nc.Block())

        def over_chunks(eng, pair):
            def chunk(c, pairs):
                pair(c, 0, False)
                with eng.Fori(1, pairs) as h:
                    pair(c, h, False)

            for c in range(3):
                chunk(c, NSUP // 2)
            with eng.Fori(3, NCH - 1) as c:
                chunk(c, NSUP // 2)
            chunk(NCH - 1, NSUP // 2 - 1)
            pair(NCH - 1, NSUP // 2 - 1, True)

        def starts(h):
            return isinstance(h, int) and h == 0

        def scanned(c, h, b):
            if isinstance(c, int) and isinstance(h, int) and (c - 1) * NSUP + 2 * h + b < 1:
                return None
            return None if isinstance(c, int) and c == 0 else (c - 1) * NSUP + 2 * h + b - 1

        @block.sync
        def _(sp):
            def load_bases(c):
                sp.dma_start(bases[0:1, bass.ds(c % 2, 1), :].rearrange("p a n -> p (a n)"),
                             dst_first[:, bass.ds(c * P, P)]).then_inc(bases_in, 16)

            def pair(c, h, last):
                if starts(h):
                    sp.wait_ge(bases_in, 16 * (c + 1))
                    if not isinstance(c, int) or c > 0:
                        load_bases(c + 1)
                for b in range(2):
                    u = c * NSUP + 2 * h + b
                    need(sp, prods_ready, NG * (u - 1))
                    sp.dma_start(idx_sb[:, b, :], idx[bass.ds(u, 1), :, :].rearrange("a p n -> (a p) n")
                                 ).then_inc(idx_in[b], 16)
                    sp.dma_start(near_sb[:, b, :].rearrange("j (r i) -> j r i", r=SUP),
                                 near_v[:, bass.ds((2 * h + b) * SUP, SUP), bass.ds(c * P, P)]
                                 ).then_inc(near_in[b], 16)
                    sp.dma_start(ea_sb[:, b, :], ea[bass.ds(u, 1), :, :].rearrange("a p n -> (a p) n")
                                 ).then_inc(ea_in[b], 16)
                    for g in range(NG):
                        _, base = nc.values_load_multi_w_load_instructions(
                            bases[0:1, bass.ds(c % 2, 1), bass.ds((2 * h + b) * SUP + g * GRP, GRP)].rearrange(
                                "p a n -> p (a n)"), engines=(mybir.EngineType.SP,),
                            min_val=0, max_val=N, skip_runtime_bounds_check_because="dst is a node's number")
                        need(sp, prods_ready, NG * (u - 1) + g + 1)
                        for j in range(GRP):
                            sp.dma_start(window[:, g, j, :], q_tab[bass.ds(base[j], P), :]
                                         ).then_inc(window_in[g], 16)

            load_bases(0)
            sp.wait_ge(bases_in, 16)
            load_bases(1)
            over_chunks(sp, pair)
            sp.wait_ge(bases_in, 16 * (NCH + 1))

        @block.gpsimd
        def _(pool):
            def pair(c, h, last):
                for b in range(2):
                    w = c * (NSUP // 2) + h
                    u = 2 * w + b
                    pool.wait_ge(idx_in[b], 16 * (w + 1))
                    for g in range(NG):
                        need(pool, prods_ready, NG * (u - 1) + g + 1)
                        pool.sem_inc(pool_turns, 1)
                        for j in range(GRP):
                            pool.indirect_dma_start(
                                out=qpair[:, g, 0, j * F:(j + 1) * F], out_offset=None, in_=q_tab,
                                in_offset=bass.IndirectOffsetOnAxis(
                                    ap=idx_sb[:, b, g * GRP + j:g * GRP + j + 1], axis=0)
                            ).then_inc(q_in[g], 16)

            over_chunks(pool, pair)

            def batch(m, b):
                need(pool, rows_used, m - 1)
                nc.gpsimd.tensor_copy(tile_b[:, b, :], tile_i[:, bass.ds(m * LB, LB)]).then_inc(tiles_copied, 1)
                pool.wait_ge(tiles_copied, m + 1)
                pool.sem_inc(pool_turns, 1)
                for j in range(LB):
                    pool.indirect_dma_start(out=rows_i[:, b, j * P:(j + 1) * P], out_offset=None, in_=dst_rows,
                                            in_offset=bass.IndirectOffsetOnAxis(ap=tile_b[:, b, j:j + 1], axis=0)
                                            ).then_inc(rows_in[b], 16)

            pool.wait_ge(tiles_ready, 1)
            for b in range(2):
                pool.wait_ge(k_ready, NG * (NCOL - 1 + b))
                batch(b, b)
            with pool.Fori(1, NB // 2) as m:
                batch(2 * m, 0)
                batch(2 * m + 1, 1)
            pool.wait_ge(rows_out, 16 * (NCOL - NSUP + 1))
            pool.indirect_dma_start(out=fix[:, :, :].rearrange("p k c -> p (k c)"), out_offset=None, in_=state,
                                    in_offset=bass.IndirectOffsetOnAxis(ap=fix_i[:, 0:1], axis=0)
                                    ).then_inc(fix_in, 16)
            batch(NB - 1, 0)
            pool.wait_ge(fixed_ready, 1)
            pool.indirect_dma_start(out=state, out_offset=bass.IndirectOffsetOnAxis(ap=fix_i[:, 0:1], axis=0),
                                    in_=fixed[:, :, :].rearrange("p k c -> p (k c)"), in_offset=None
                                    ).then_inc(fix_out, 16)
            pool.wait_ge(fix_out, 16)

        @block.tensor
        def _(pe):
            def squares(n, w, b, g):
                if g == 0:
                    pe.wait_ge(near_in[b], 16 * (w + 1))
                need(pe, onehot_ready, n - 1)
                nc.tensor.matmul(sq_ps[:, g % 2, :], square_sb[:, :], near_sb[:, b, g * GRP * P:(g + 1) * GRP * P],
                                 start=True, stop=True).then_inc(squares_ready, 1)

            def keys(n, w, b, g):
                if g == 0:
                    pe.wait_ge(ea_in[b], 16 * (w + 1))
                need(pe, prods_ready, n - 1)
                nc.tensor.matmul(k_ps[:, g % 2, :], ones3_sb[:, :], bk3_sb[:, :], start=True, stop=False,
                                 skip_group_check=True)
                for j in range(GRP):
                    t = g * GRP + j
                    m = nc.tensor.matmul(k_ps[:, g % 2, j * F:(j + 1) * F], ea_sb[:, b, t * P:(t + 1) * P],
                                         wk_sb[:, :], start=False, stop=True, skip_group_check=True)
                m.then_inc(k_ready, 1)

            def pick(n, u, g):
                pe.wait_ge(window_in[g], 16 * GRP * (u + 1))
                need(pe, qd_copied, n - 1)
                pe.wait_ge(onehot_ready, n + 1)
                for j in range(GRP):
                    m = nc.tensor.matmul(qd_ps[:, g % 2, j * F:(j + 1) * F], onehot[:, g % 2, j * P:(j + 1) * P],
                                         window[:, g, j, :], start=True, stop=True)
                m.then_inc(qd_ready, 1)

            def turn(v):
                pe.wait_ge(staged_ready, v + 1)
                for j in range(CPS):
                    t = nc.tensor.transpose(t_ps[:, j, :], staged[:, j, :], ident[:, :])
                t.then_inc(turned, 1)

            def pair(c, h, last):
                w = c * (NSUP // 2) + h
                n = 2 * NG * w
                for b in range(2):
                    for g in range(NG):
                        m = NG * b + g
                        m2, m1 = m + 2, m + 1
                        if not (last and m2 >= 2 * NG):
                            squares(n + m2, w + m2 // (2 * NG), m2 // NG % 2, m2 % NG)
                        keys(n + m, w, b, g)
                        if not (last and m1 >= 2 * NG):
                            pick(n + m1, 2 * w + m1 // NG, m1 % NG)
                        if g == 0 and scanned(c, h, b) is not None:
                            turn(scanned(c, h, b))

            squares(0, 0, 0, 0)
            squares(1, 0, 0, 1)
            pick(0, 0, 0)
            over_chunks(pe, pair)
            with pe.Fori(NCOL - NSUP - 1, NCOL) as v:
                turn(v)
            pe.wait_ge(prods_ready, NG * NCOL)
            pe.wait_ge(rows_ready, NCOL + 1)
            for k in range(3):
                nc.tensor.transpose(k_ps[0:CH, 0, k * P:(k + 1) * P],
                                    rows[:, (NCH - 1) % 2, P - 1, k * CH:(k + 1) * CH], ident[:, :])
            pe.wait_ge(pens_ready, 2)
            for k in range(2):
                t = nc.tensor.transpose(k_ps[0:CH, 1, k * P:(k + 1) * P], pens[:, k, :], ident[:, :])
            t.then_inc(ends_turned, 1)
            pe.wait_ge(carry_ready, 3)
            pe.wait_ge(qd_copied, NG * NCOL)
            for k in range(3):
                t = nc.tensor.transpose(qd_ps[:, 0, k * CH:(k + 1) * CH], carry_t[:, k, :], ident[0:CH, 0:CH])
            t.then_inc(carry_turned, 1)

        @block.scalar
        def _(act):
            def pick_mask(n, g):
                act.wait_ge(squares_ready, n + 1)
                need(act, qd_ready, n - 1)
                nc.scalar.activation(onehot[:, g % 2, :], sq_ps[:, g % 2, :], ACT.Relu, bias=1.0, scale=-1.0
                                     ).then_inc(onehot_ready, 1)

            def take_qd(n, g):
                act.wait_ge(qd_ready, n + 1)
                need(act, prods_ready, n - NG + 1)
                nc.scalar.copy(qpair[:, g, 1, :], qd_ps[:, g % 2, :]).then_inc(qd_copied, 1)

            def count_tiles(u):
                need(act, signs_ready, u)
                nc.scalar.activation(sign_out[:, :], first_f[:, :], ACT.Sign, bias=nidh[:, bass.ds(u, 1)],
                                     scale=-1.0, accum_out=signs[:, bass.ds(u, 1)]).then_inc(signs_ready, 1)

            def stage(v):
                c, s = v // NSUP, v % NSUP
                act.wait_ge(logits_ready, NG * NSUP * (c + 1))
                nc.scalar.copy(staged[:, :, :],
                               logits[:, bass.ds(c % 2, 1), bass.ds(s * CPS, CPS), :].rearrange(
                                   "p a c i -> p (a c) i")).then_inc(staged_ready, 1)
                nc.scalar.copy(pen3[:, :, 1:W1],
                               pen[:, None, bass.ds(c * P, P)].to_broadcast([P, CPS, P]))
                act.wait_ge(rows_ready, v + 1)
                nc.scalar.copy(terms[:, 1:4, :, 0:1].rearrange("p k c o -> p k (c o)"),
                               rows[:, bass.ds((c + 1) % 2, 1), P - 1, :].rearrange("p a (k c) -> p (a k) c", k=3)[
                                   :, :, bass.ds(s * CPS, CPS)])

            def take_turned(v):
                act.wait_ge(turned, v + 1)
                nc.scalar.copy(terms[:, 1, :, 1:W1], t_ps[:, 0:CPS, :]).then_inc(terms_ready, 1)

            def exps(v):
                act.wait_ge(diffs_ready, v + 1)
                nc.scalar.activation(terms[:, 0:3:2, :, 1:W1], diffs[:, :, :, :], ACT.Exp, scale=SCALE
                                     ).then_inc(exps_ready, 1)

            def take_sums(v):
                c, s = v // NSUP, v % NSUP
                act.wait_ge(sums_ready, v + 1)
                nc.scalar.copy(
                    rows[:, bass.ds(c % 2, 1), :, :].rearrange("p a i (k c) -> p (a k) c i", k=3)[
                        :, :, bass.ds(s * CPS, CPS), :],
                    sums[:, :, :, 1:W1]).then_inc(rows_ready, 1)

            def pair(c, h, last):
                w = c * (NSUP // 2) + h
                n = 2 * NG * w

                def masks_and_copies(m):
                    m2, m1 = m + 2, m + 1
                    if not (last and m2 >= 2 * NG):
                        pick_mask(n + m2, m2 % NG)
                    if not (last and m1 >= 2 * NG):
                        take_qd(n + m1, m1 % NG)

                for b in range(2):
                    v = scanned(c, h, b)
                    if v is not None:
                        stage(v)
                    masks_and_copies(NG * b)
                    if v is not None:
                        take_turned(v)
                        exps(v)
                    masks_and_copies(NG * b + 1)
                    count_tiles(2 * w + b)
                    masks_and_copies(NG * b + 2)
                    masks_and_copies(NG * b + 3)
                    if v is not None:
                        if not isinstance(c, int) or c > 2 or (c == 2 and (not starts(h) or b > 0)):
                            need(act, rows_out, 16 * (v - NSUP))
                            take_sums(v)
                            store(v - NSUP)
                        else:
                            take_sums(v)

            def store(m):
                c, part = m // NSUP, m % NSUP
                act.wait_ge(rows_ready, NSUP * (c + 1) + 1)
                act.dma_start(state_v[:, bass.ds((c * P + part * SUP) * ROW, SUP * ROW)],
                              rows[:, bass.ds(c % 2, 1), bass.ds(part * SUP, SUP), :].rearrange("p a i r -> p (a i r)")
                              ).then_inc(rows_out, 16)

            def unit(v):
                stage(v)
                take_turned(v)
                exps(v)
                act.wait_ge(rows_out, 16 * (v - NSUP))
                take_sums(v)

            act.wait_ge(ones_ready, 2)
            pick_mask(0, 0)
            pick_mask(1, 1)
            take_qd(0, 0)
            over_chunks(act, pair)
            with act.Fori(NCOL - NSUP - 1, NCOL) as v:
                unit(v)
                store(v - NSUP)
            act.wait_ge(rows_ready, NCOL + 1)
            act.wait_ge(rows_out, 16 * (NCOL - NSUP))
            act.dma_start(state_v[:, (NCH - 1) * P * ROW:NCH * P * ROW],
                          rows[:, (NCH - 1) % 2, :, :].rearrange("p i r -> p (i r)")).then_inc(rows_out, 16)
            act.wait_ge(diff_ready, 1)
            nc.scalar.activation(fac, diff, ACT.Exp, scale=SCALE).then_inc(fac_ready, 1)
            act.wait_ge(cdiff_ready, 1)
            nc.scalar.activation(cfac[:, :, :], cdiff[:, :, :], ACT.Exp, scale=SCALE).then_inc(cfac_ready, 1)
            act.wait_ge(rows_out, 16 * (NCOL - NSUP + 1))

        @block.vector
        def _(dve):
            nc.vector.memset(rows[:, 1, P - 1, 0:CH], -BIG)
            nc.vector.memset(rows[:, 1, P - 1, CH:ROW], 0.0).then_inc(rows_ready, 1)
            nc.vector.memset(pen3[:, :, 0:1], -BIG).then_inc(ones_ready, 1)
            nc.vector.memset(terms[:, 0, :, 0:1], 0.0).then_inc(ones_ready, 1)

            def products(c, h, b, g):
                u = c * NSUP + 2 * h + b
                n = NG * u + g
                dve.wait_ge(q_in[g], 16 * GRP * (u + 1))
                need(dve, logits_ready, n - 1)
                dve.wait_ge(k_ready, n + 1)
                dve.wait_ge(qd_copied, n + 1)
                nc.vector.tensor_tensor(prod[:, g % 2, 0:2, :],
                                        k_ps[:, g % 2, :].unsqueeze(1).to_broadcast([P, 2, GRP * F]),
                                        qpair[:, g, :, :], ALU.mult)
                nc.vector.tensor_tensor(prod[:, g % 2, 2, :], qpair[:, g, 0, :], qpair[:, g, 1, :], ALU.mult
                                        ).then_inc(prods_ready, 1)

            def logits_of(c, h, b, g):
                dve.wait_ge(prods_ready, NG * (c * NSUP + 2 * h + b) + g + 1)
                if starts(h) and b + g == 0 and (not isinstance(c, int) or c > 1):
                    dve.wait_ge(staged_ready, NSUP * (c - 1))
                o = logits[:, bass.ds(c % 2, 1), :, bass.ds((2 * h + b) * SUP + g * GRP, GRP)].rearrange(
                    "p o (a c) r -> p (o a) r c", a=3)
                nc.vector.tensor_reduce(o, prod[:, g % 2, :, :].rearrange("p a (r c d) -> p a r c d", r=GRP, d=D),
                                        AX_X, ALU.add).then_inc(logits_ready, 1)

            def running_max(v):
                dve.wait_ge(rows_ready, v + 1)
                dve.wait_ge(terms_ready, v + 1)
                nc.vector.tensor_tensor_scan(sums[:, 0, :, :].rearrange("p c i -> p (c i)"),
                                             pen3[:, :, :].rearrange("p c i -> p (c i)"),
                                             terms[:, 1, :, :].rearrange("p c i -> p (c i)"), -BIG, ALU.add, ALU.max
                                             ).then_inc(max_ready, 1)
                dve.wait_ge(max_ready, v + 1)
                nc.vector.tensor_tensor(shifted[:, :, :], sums[:, 0, :, 0:P], pen3[:, :, 1:W1], ALU.add
                                        ).then_inc(shift_ready, 1)
                nc.vector.tensor_tensor(diffs[:, 1, :, :], terms[:, 1, :, 1:W1], sums[:, 0, :, 1:W1], ALU.subtract)
                dve.wait_ge(shift_ready, v + 1)
                nc.vector.tensor_tensor(diffs[:, 0, :, :], shifted[:, :, :], sums[:, 0, :, 1:W1], ALU.subtract
                                        ).then_inc(diffs_ready, 1)

            def running_sums(v):
                dve.wait_ge(exps_ready, v + 1)
                nc.vector.tensor_tensor(terms[:, 3, :, 1:W1], terms[:, 2, :, 1:W1],
                                        att[:, None, bass.ds(v // NSUP * P, P)].to_broadcast([P, CPS, P]), ALU.mult
                                        ).then_inc(weighted_ready, 1)
                dve.wait_ge(weighted_ready, v + 1)
                for k in (1, 2):
                    s = nc.vector.tensor_tensor_scan(sums[:, k, :, :].rearrange("p c i -> p (c i)"),
                                                     terms[:, 0, :, :].rearrange("p c i -> p (c i)"),
                                                     terms[:, k + 1, :, :].rearrange("p c i -> p (c i)"), 0.0,
                                                     ALU.mult, ALU.add)
                s.then_inc(sums_ready, 1)

            def find_tiles():
                dve.wait_ge(signs_ready, NN)
                nc.vector.tensor_scalar(last_f[:, :], signs[:, 0:NN], 0.5, T // 2 - 1.0, ALU.mult, ALU.add
                                        ).then_inc(step, 1)
                dve.wait_ge(step, 1)
                nc.vector.tensor_scalar(tile_f[:, :], last_f[:, :], 0.0, None, ALU.max).then_inc(step, 1)
                dve.wait_ge(step, 2)
                nc.vector.tensor_copy(tile_i[:, :], tile_f[:, :]).then_inc(tiles_ready, 1)

            def pair(c, h, last):
                if last:
                    find_tiles()
                for b in range(2):
                    v = scanned(c, h, b)
                    for g in range(NG):
                        products(c, h, b, g)
                        if g > 0:
                            logits_of(c, h, b, g - 1)
                        elif b > 0:
                            logits_of(c, h, b - 1, NG - 1)
                        if v is not None and g == 0:
                            running_max(v)
                        if v is not None and g == 2:
                            running_sums(v)
                logits_of(c, h, 1, NG - 1)

            over_chunks(dve, pair)

            le = prod[:, 0, 0:3, :].rearrange("p a n -> p (a n)")[:, 0:LB * P].rearrange("p (l i) -> p l i", i=P)

            def count(m):
                b = m % 2
                dve.wait_ge(rows_in[b], 16 * LB * (m // 2 + 1))
                need(dve, rows_used, m)
                nc.vector.tensor_tensor(le, rows_i[:, b, :].rearrange("p (l i) -> p l i", i=P),
                                        nid[:, m * LB:(m + 1) * LB].unsqueeze(2).to_broadcast([P, LB, P]), ALU.is_le
                                        ).then_inc(le_ready, 1)
                dve.wait_ge(le_ready, m + 1)
                nc.vector.tensor_reduce(cnt[:, m * LB:(m + 1) * LB], le, AX_X, ALU.add).then_inc(rows_used, 1)

            def join_ends():
                dve.wait_ge(ends_turned, 1)
                nc.vector.tensor_copy(ends[:, 0:3, :], k_ps[0:CH, 0, 0:3 * P].rearrange("p (k n) -> p k n", k=3))
                nc.vector.tensor_copy(ends[:, 3:5, :], k_ps[0:CH, 1, 0:2 * P].rearrange("p (k n) -> p k n", k=2)
                                      ).then_inc(join_step, 1)
                dve.wait_ge(join_step, 1)
                nc.vector.tensor_tensor_scan(open_[:, 0, 1:W1], ends[:, 3, :], ends[:, 0, :], -BIG, ALU.add, ALU.max
                                             ).then_inc(join_step, 1)
                dve.wait_ge(join_step, 2)
                nc.vector.tensor_tensor(diff[:, 0, :], open_[:, 0, 0:P], ends[:, 3, :], ALU.add
                                        ).then_inc(join_step, 1)
                nc.vector.tensor_tensor(diff[:, 1, :], ends[:, 0, :], open_[:, 0, 1:W1], ALU.subtract)
                dve.wait_ge(join_step, 3)
                nc.vector.tensor_tensor(diff[:, 0, :], diff[:, 0, :], open_[:, 0, 1:W1], ALU.subtract
                                        ).then_inc(diff_ready, 1)
                dve.wait_ge(fac_ready, 1)
                for k in range(2):
                    m = nc.vector.tensor_tensor(scaled[:, k, :], ends[:, 1 + k, :], fac[:, 1, :], ALU.mult)
                m.then_inc(join_step, 1)
                dve.wait_ge(join_step, 4)
                for k in range(2):
                    m = nc.vector.tensor_tensor_scan(open_[:, 1 + k, 1:W1], fac[:, 0, :], scaled[:, k, :], 0.0,
                                                     ALU.mult, ALU.add)
                m.then_inc(join_step, 1)
                dve.wait_ge(join_step, 5)
                nc.vector.tensor_tensor(carry_t[:, 0, :], open_[:, 0, 0:P], ends[:, 4, :], ALU.add
                                        ).then_inc(carry_ready, 1)
                for k in (1, 2):
                    nc.vector.tensor_copy(carry_t[:, k, :], open_[:, k, 0:P]).then_inc(carry_ready, 1)
                dve.wait_ge(carry_turned, 1)
                nc.vector.tensor_copy(carry[:, :, :], qd_ps[:, 0, 0:ROW].rearrange("p (k c) -> p k c", k=3)
                                      ).then_inc(join_step, 1)

            def join_fix():
                dve.wait_ge(join_step, 6)
                dve.wait_ge(fix_in, 16)
                nc.vector.tensor_tensor(best[:, :], carry[:, 0, :], fix[:, 0, :], ALU.max).then_inc(join_step, 1)
                dve.wait_ge(join_step, 7)
                nc.vector.tensor_tensor(cdiff[:, 0, :], carry[:, 0, :], best[:, :], ALU.subtract)
                nc.vector.tensor_tensor(cdiff[:, 1, :], fix[:, 0, :], best[:, :], ALU.subtract
                                        ).then_inc(cdiff_ready, 1)
                dve.wait_ge(cfac_ready, 1)
                for k in range(2):
                    nc.vector.tensor_tensor(part[:, k, 0, :], carry[:, 1 + k, :], cfac[:, 0, :], ALU.mult)
                    m = nc.vector.tensor_tensor(part[:, k, 1, :], fix[:, 1 + k, :], cfac[:, 1, :], ALU.mult)
                m.then_inc(join_step, 1)
                dve.wait_ge(join_step, 8)
                nc.vector.tensor_copy(fixed[:, 0, :], best[:, :])
                nc.vector.tensor_tensor(fixed[:, 1:3, :], part[:, :, 0, :], part[:, :, 1, :], ALU.add
                                        ).then_inc(fixed_ready, 1)

            nc.vector.tensor_copy(pens[:, 0, :], whole_pen[:, 0:1].to_broadcast([P, CH])).then_inc(pens_ready, 1)
            nc.vector.tensor_copy(pens[:, 1, :], cont_pen[:, 0:1].to_broadcast([P, CH])).then_inc(pens_ready, 1)
            nc.vector.memset(open_[:, 0, 0:1], -BIG)
            nc.vector.memset(open_[:, 1:3, 0:1], 0.0)
            dve.wait_ge(logits_ready, NG * NCOL)
            for k in range(NSUP + 1):
                running_max(NCOL - NSUP - 1 + k)
                running_sums(NCOL - NSUP - 1 + k)
                if k % 2:
                    count(k // 2)
            count(4)
            join_ends()
            for m in range(5, NB - 1):
                count(m)
            join_fix()
            count(NB - 1)
            dve.wait_ge(rows_used, NB)
            nc.vector.scalar_tensor_tensor(out=last_f[:, :], in0=tile_f[:, :], scalar=float(P), in1=cnt[:, :],
                                           op0=ALU.mult, op1=ALU.add).then_inc(step, 1)
            dve.wait_ge(step, 3)
            nc.vector.tensor_tensor(has[:, :], last_f[:, 1:NN], last_f[:, 0:NT], ALU.is_gt)
            nc.vector.tensor_scalar(last_i[:, :], last_f[:, :], -1.0, 0.0, ALU.add, ALU.max).then_inc(step, 1)


def out_pass(nc, env):
    ident, last_i, has, state, x_v, v_v, out_v = (env[k] for k in (
        "ident", "last_i", "has", "state", "x_v", "v_v", "out_v"))
    with ExitStack() as ctx:
        def sb(name, shape, dt=F32):
            return ctx.enter_context(nc.sbuf_tensor(name, shape, dt))

        def psum(name, shape):
            return ctx.enter_context(nc.psum_tensor(name, shape, F32))

        def sem(name):
            return ctx.enter_context(nc.semaphore(name))

        wo_sb = sb("wo_sb", [P, F])
        bo_sb = sb("bo_sb", [P, F])
        xs = sb("xs2", [P, 2, HALF, F])
        vs = sb("vs2", [P, 2, HALF, F])
        last_b = sb("last_b", [P, 2, HALF], I32)
        st = sb("st", [P, 2, HALF, 3, CH])
        rden = sb("rden", [P, HALF, CH])
        ratio = sb("ratio", [P, HALF, CH])
        score = sb("score", [P, HALF, H])
        score_m = sb("score_m", [P, HALF, H])
        hv = sb("hv", [P, 2, HALF, F])
        hvT = sb("hvT", [P, 2, HALF, P])
        z = sb("z", [P, HALF, F])
        y = sb("y", [P, HALF, F])
        res = sb("res", [P, 2, HALF, F])
        hT_ps = psum("hT_ps2", [P, 2, 8, P])
        z_ps = psum("z_ps", [P, 2, 8, P])

        wo_in = sem("wo_in")
        in_sem = [sem("in0"), sem("in1")]
        batch_ready = sem("batch_ready2")
        pool_turns = sem("pool_turns2")
        st_in = [sem("st_in0"), sem("st_in1")]
        step = [sem(f"node_step{i}") for i in range(4)]
        hv_ready = sem("hv_ready")
        hvT_ready = sem("hvT_ready")
        hvT_copied = sem("hvT_copied")
        z_ready = sem("z_ready")
        z_step = sem("z_step")
        y_step = sem("y_step")
        res_ready = sem("res_ready")
        res_out = [sem("res_out0"), sem("res_out1")]
        block = ctx.enter_context(nc.Block())

        @block.sync
        def _(sp):
            def load(w):
                for b in range(2):
                    k = 2 * w + b
                    need(sp, res_ready, k - 1)
                    sp.dma_start(xs[:, b, :, :], x_v[:, bass.ds(k * HALF * F, HALF * F)]).then_inc(in_sem[b], 16)
                    sp.dma_start(vs[:, b, :, :], v_v[:, bass.ds(k * HALF * F, HALF * F)]).then_inc(in_sem[b], 16)

            sp.dma_start(wo_sb[:, :], env["woT"]).then_inc(wo_in, 16)
            sp.dma_start(bo_sb[:, :], env["bo"].to_broadcast([P, F])).then_inc(wo_in, 16)
            load(0)
            with sp.Fori(1, NSTEP // 2) as w:
                load(w)

        @block.gpsimd
        def _(pool):
            with pool.Fori(0, NSTEP // 2) as w:
                for b in range(2):
                    pool.wait_ge(batch_ready, 2 * w + b + 1)
                    pool.sem_inc(pool_turns, 1)
                    for j in range(HALF):
                        pool.indirect_dma_start(out=st[:, b, j, :, :].rearrange("p k c -> p (k c)"), out_offset=None,
                                                in_=state,
                                                in_offset=bass.IndirectOffsetOnAxis(ap=last_b[:, b, j:j + 1], axis=0)
                                                ).then_inc(st_in[b], 16)

        @block.tensor
        def _(pe):
            def turn(k, b):
                pe.wait_ge(hv_ready, k + 1)
                for j in range(HALF):
                    t = nc.tensor.transpose(hT_ps[:, b, j, :], hv[:, b, j, :], ident[:, :])
                t.then_inc(hvT_ready, 1)

            def project(k, b):
                pe.wait_ge(hvT_copied, k + 1)
                need(pe, z_step, k - 1)
                for j in range(HALF):
                    m = nc.tensor.matmul(z_ps[:, b, j, :], hvT[:, b, j, :], wo_sb[:, :], start=True, stop=True)
                m.then_inc(z_ready, 1)

            pe.wait_ge(wo_in, 32)
            turn(0, 0)
            project(0, 0)
            turn(1, 1)
            project(1, 1)
            with pe.Fori(1, NSTEP // 2) as w:
                for b in range(2):
                    turn(2 * w + b, b)
                    project(2 * w + b, b)

        @block.scalar
        def _(act):
            def copy(k, b):
                act.wait_ge(hvT_ready, k + 1)
                nc.scalar.copy(hvT[:, b, :, :], hT_ps[:, b, 0:HALF, :]).then_inc(hvT_copied, 1)

            def store(k, b):
                act.wait_ge(res_ready, k + 1)
                act.dma_start(out_v[:, bass.ds(k * HALF * F, HALF * F)], res[:, b, :, :]).then_inc(res_out[b], 16)

            copy(0, 0)
            copy(1, 1)
            store(0, 0)
            with act.Fori(1, NSTEP // 2) as w:
                copy(2 * w, 0)
                store(2 * w - 1, 1)
                copy(2 * w + 1, 1)
                store(2 * w, 0)
            store(NSTEP - 1, 1)
            for b in range(2):
                act.wait_ge(res_out[b], 16 * (NSTEP // 2))

        @block.vector
        def _(dve):
            def hand_over(k, b):
                nc.vector.tensor_copy(last_b[:, b, :], last_i[:, bass.ds(k * HALF + 1, HALF)]
                                      ).then_inc(batch_ready, 1)

            def scores(k, w, b):
                dve.wait_ge(st_in[b], 16 * HALF * (w + 1))
                nc.vector.reciprocal(rden[:, :, :], st[:, b, :, 1, :]).then_inc(step[0], 1)
                dve.wait_ge(step[0], k + 1)
                nc.vector.tensor_tensor(ratio[:, :, :], st[:, b, :, 2, :], rden[:, :, :], ALU.mult
                                        ).then_inc(step[1], 1)
                dve.wait_ge(step[1], k + 1)
                nc.vector.tensor_reduce(score[:, :, :], ratio[:, :, :].rearrange("p t (a h) -> p t h a", a=3), AX_X,
                                        ALU.add).then_inc(step[2], 1)
                dve.wait_ge(step[2], k + 1)
                nc.vector.tensor_tensor(score_m[:, :, :], score[:, :, :],
                                        has[:, bass.ds(k * HALF, HALF)].unsqueeze(2).to_broadcast([P, HALF, H]),
                                        ALU.mult).then_inc(step[3], 1)
                dve.wait_ge(step[3], k + 1)
                dve.wait_ge(in_sem[b], 32 * (w + 1))
                nc.vector.tensor_tensor(hv[:, b, :, :].rearrange("p t (h d) -> p (t h) d", h=H),
                                        vs[:, b, :, :].rearrange("p t (h d) -> p (t h) d", h=H),
                                        score_m[:, :, :].rearrange("p t h -> p (t h)").unsqueeze(2).to_broadcast(
                                            [P, HALF * H, D]),
                                        ALU.mult).then_inc(hv_ready, 1)

            def finish(k, w, b):
                dve.wait_ge(z_ready, k + 1)
                nc.vector.tensor_tensor(z[:, :, :], z_ps[:, b, 0:HALF, :],
                                        bo_sb[:, None, :].to_broadcast([P, HALF, F]), ALU.add).then_inc(z_step, 1)
                dve.wait_ge(z_step, k + 1)
                nc.vector.scalar_tensor_tensor(out=y[:, :, :], in0=z[:, :, :], scalar=SLOPE, in1=z[:, :, :],
                                               op0=ALU.mult, op1=ALU.max).then_inc(y_step, 1)
                dve.wait_ge(y_step, k + 1)
                need(dve, res_out[b], 16 * w)
                nc.vector.tensor_tensor(res[:, b, :, :], y[:, :, :], xs[:, b, :, :], ALU.add).then_inc(res_ready, 1)

            dve.wait_ge(wo_in, 32)
            hand_over(0, 0)
            hand_over(1, 1)
            scores(0, 0, 0)
            hand_over(2, 0)
            scores(1, 0, 1)
            hand_over(3, 1)
            finish(0, 0, 0)
            with dve.Fori(1, NSTEP // 2 - 1) as w:
                scores(2 * w, w, 0)
                hand_over(2 * w + 2, 0)
                finish(2 * w - 1, w - 1, 1)
                scores(2 * w + 1, w, 1)
                hand_over(2 * w + 3, 1)
                finish(2 * w, w, 0)
            scores(NSTEP - 2, NSTEP // 2 - 1, 0)
            finish(NSTEP - 3, NSTEP // 2 - 2, 1)
            scores(NSTEP - 1, NSTEP // 2 - 1, 1)
            finish(NSTEP - 2, NSTEP // 2 - 1, 0)
            finish(NSTEP - 1, NSTEP // 2 - 1, 1)


def kernel(**inputs):
    import ml_dtypes
    import numpy as np
    import concourse.bacc as bacc
    from concourse.bass_utils import run_bass_kernel_spmd

    def padded(a, rows, value):
        tail = np.full((rows - a.shape[0],) + a.shape[1:], value, a.dtype)
        return np.concatenate([a, tail])

    g = {k: np.asarray(v) for k, v in inputs.items()}
    src = padded(g["src"], EPAD, 0)
    dst = padded(g["dst"], EPAD, N)
    before = np.concatenate([np.full(1, -1, dst.dtype), dst[:-1]])

    one, at = np.ones(P, np.int64), np.arange(P)

    def by_tile(a):
        return a.reshape(NSUP, SUP, NCH, P).transpose(2, 0, 3, 1).reshape(NCH * NSUP, P, SUP)

    ea = padded(g["edge_attr_128"], EPAD, 0).reshape(NSUP, SUP, NCH, P, F).transpose(2, 0, 4, 1, 3)
    arrays = {
        "x": padded(g["x"], NPAD, 0),
        "idx": by_tile(src),
        "dst_rows": dst.reshape(P * NCH, P),
        "dst_prev": before.reshape(P, T),
        "dst_first": padded(dst[::P].reshape(P, NCH).T.reshape(NCH * P), (NCH + 2) * P, N).reshape(1, (NCH + 2) * P),
        "ea": ea.reshape(NCH * NSUP, F, SUP * P),
        "dist": padded(g["edge_weight1"], EPAD, 1).reshape(P, T),
        "wqvT": np.concatenate([g["L0_gnn_Wq"].T, g["L0_gnn_Wv"].T], axis=1),
        "bqv": np.concatenate([g["L0_gnn_bq"], g["L0_gnn_bv"]]).reshape(1, 2 * F),
        "wkT": g["L0_gnn_Wk"].T,
        "bk": g["L0_gnn_bk"].reshape(1, F),
        "woT": g["L0_gnn_Wo"].T,
        "bo": g["L0_gnn_bo"].reshape(1, F),
        "lam": g["L0_gnn_lam"].reshape(1, 1),
        "ident": np.eye(P, dtype=np.float32),
        "iota": np.concatenate([np.arange(P)[:, None] * NT + np.arange(-1, NCOL - 1)[None, :],
                                np.arange(P)[:, None] * T - 1], axis=1).astype(np.float32),
        "square": np.stack([one, one, -2 * one * at, at * at // 256 * 256, at * at % 256]).astype(ml_dtypes.bfloat16),
    }
    nc = bacc.Bacc("TRN2", target_bir_lowering=False, num_devices=1)
    feeds, args = {}, []
    for name, a in arrays.items():
        a = np.ascontiguousarray(a)
        feeds[f"in_{name}"] = a
        args.append(nc.dram_tensor(f"in_{name}", a.shape, mybir.dt.from_np(a.dtype), kind="ExternalInput").ap())
    args.append(nc.dram_tensor("out_0", (NPAD, F), F32, kind="ExternalOutput").ap())
    gnn_kernel(nc, *args)
    r = run_bass_kernel_spmd(nc, [feeds], core_ids=[0])
    return r.results[0]["out_0"][:N]
```
